# Optimizing a Trainium2 kernel written in Bass

```python
import numpy as np
import jax
import jax.numpy as jnp

def _softmax(x, axis=-1):
    return jax.nn.softmax(x, axis=axis)

def _gelu(x):
    return jax.nn.gelu(x, approximate=True)

def _silu(x):
    return jax.nn.silu(x)

def _sigmoid(x):
    return jax.nn.sigmoid(x)

def _layernorm(x, axis=-1, eps=1e-05):
    m = jnp.mean(x, axis=axis, keepdims=True)
    v = jnp.var(x, axis=axis, keepdims=True)
    return (x - m) / jnp.sqrt(v + eps)

def _scatter_add(tgt, idx, src, axis=0):
    return tgt.at[idx].add(src)

def _segment_sum(src, seg, n):
    return jax.ops.segment_sum(src, seg, n)
kernel_name = 'mk_seq_postln_d1_jaxref_r8_a4fd52'

def setup_inputs(seed: int=0):
    np.random.seed(seed)
    _w = jnp.asarray

    def _L0_attn_setup():
        import jax, jax.numpy as jnp
        import numpy as np
        NUM_HEADS = 16
        EPS = 1e-06
        CHUNK = 128
        key = jax.random.key(seed)
        ks = jax.random.split(key, 6)
        B, T, E = (4, 256, 128)
        s = 0.02
        x = jax.random.normal(ks[0], (B, T, E), jnp.float32)
        Wq = jax.random.normal(ks[1], (E, E), jnp.float32) * s
        Wk = jax.random.normal(ks[2], (E, E), jnp.float32) * s
        Wv = jax.random.normal(ks[3], (E, E), jnp.float32) * s
        Wp = jax.random.normal(ks[4], (E, E), jnp.float32) * s
        bp = jnp.zeros((E,), jnp.float32)
        return {'x': x, 'Wq': Wq, 'Wk': Wk, 'Wv': Wv, 'Wp': Wp, 'bp': bp}
    _L0_attn_in = _L0_attn_setup()

    def _L0_ffn_setup():
        import jax, jax.numpy as jnp
        import numpy as np
        DIM = 128

        def _reference_tuple_inner(x, W_r, W_k, W_v, mu_r, mu_k):
            B, T, C = x.shape
            x_prev = jnp.concatenate([jnp.zeros((B, 1, C), x.dtype), x[:, :-1, :]], axis=1)
            xr = mu_r * x + (1.0 - mu_r) * x_prev
            xk = mu_k * x + (1.0 - mu_k) * x_prev
            r = jax.nn.sigmoid(jnp.einsum('btc,dc->btd', xr, W_r))
            k = jnp.einsum('btc,dc->btd', xk, W_k)
            k_act = jnp.square(jax.nn.relu(k))
            out = r * jnp.einsum('btc,dc->btd', k_act, W_v)
            new_state = x[:, -1, :]
            return (out, new_state)
        key = jax.random.key(seed)
        ks = jax.random.split(key, 6)
        B, T, C = (8, 256, DIM)
        x = jax.random.normal(ks[0], (B, T, C), dtype=jnp.float32)
        s = 1.0 / np.sqrt(C)
        W_r = jax.random.uniform(ks[1], (C, C), jnp.float32, -s, s)
        W_k = jax.random.uniform(ks[2], (C, C), jnp.float32, -s, s)
        W_v = jax.random.uniform(ks[3], (C, C), jnp.float32, -s, s)
        mu_r = jax.random.uniform(ks[4], (C,), jnp.float32)
        mu_k = jax.random.uniform(ks[5], (C,), jnp.float32)
        return {'x': x, 'W_r': W_r, 'W_k': W_k, 'W_v': W_v, 'mu_r': mu_r, 'mu_k': mu_k}
    _L0_ffn_in = _L0_ffn_setup()
    _d = {'L0_attn_x': _L0_attn_in['x'], 'L0_attn_Wq': _L0_attn_in['Wq'], 'L0_attn_Wk': _L0_attn_in['Wk'], 'L0_attn_Wv': _L0_attn_in['Wv'], 'L0_attn_Wp': _L0_attn_in['Wp'], 'L0_attn_bp': _L0_attn_in['bp'], 'L0_ffn_W_r': _L0_ffn_in['W_r'], 'L0_ffn_W_k': _L0_ffn_in['W_k'], 'L0_ffn_W_v': _L0_ffn_in['W_v'], 'L0_ffn_mu_r': _L0_ffn_in['mu_r'], 'L0_ffn_mu_k': _L0_ffn_in['mu_k']}
    _x0 = _d['L0_attn_x']
    _d['L0_attn_x'] = jax.random.normal(jax.random.fold_in(jax.random.key(seed), 1), (16, 512, 128), dtype=_x0.dtype)
    del _x0
    return _d

def reference(L0_attn_x, L0_attn_Wq, L0_attn_Wk, L0_attn_Wv, L0_attn_Wp, L0_attn_bp, L0_ffn_W_r, L0_ffn_W_k, L0_ffn_W_v, L0_ffn_mu_r, L0_ffn_mu_k):

    def _L0_attn_ref(x, Wq, Wk, Wv, Wp, bp):
        import jax, jax.numpy as jnp
        import numpy as np
        NUM_HEADS = 16
        EPS = 1e-06
        CHUNK = 128
        B, T, E = x.shape
        H = NUM_HEADS
        D = E // H
        N = T // CHUNK
        q = x @ Wq.T
        k = x @ Wk.T
        v = x @ Wv.T

        def split_heads(t):
            return t.reshape(B, T, H, D).transpose(0, 2, 1, 3).reshape(B, H, N, CHUNK, D)
        phi_q = jax.nn.elu(split_heads(q)) + 1.0
        phi_k = jax.nn.elu(split_heads(k)) + 1.0
        vh = split_heads(v)
        kv = jnp.einsum('bhncd,bhnce->bhnde', phi_k, vh)
        zk = phi_k.sum(axis=3)
        S_prev = jnp.concatenate([jnp.zeros_like(kv[:, :, :1]), jnp.cumsum(kv, axis=2)[:, :, :-1]], axis=2)
        Z_prev = jnp.concatenate([jnp.zeros_like(zk[:, :, :1]), jnp.cumsum(zk, axis=2)[:, :, :-1]], axis=2)
        A = jnp.einsum('bhncd,bhnsd->bhncs', phi_q, phi_k)
        mask = jnp.tril(jnp.ones((CHUNK, CHUNK), bool))
        A = jnp.where(mask, A, 0.0)
        num = jnp.einsum('bhncs,bhnse->bhnce', A, vh) + jnp.einsum('bhncd,bhnde->bhnce', phi_q, S_prev)
        den = A.sum(-1) + jnp.einsum('bhncd,bhnd->bhnc', phi_q, Z_prev) + EPS
        y = num / den[..., None]
        y = y.reshape(B, H, T, D).transpose(0, 2, 1, 3).reshape(B, T, E)
        return y @ Wp.T + bp

    def _L0_ffn_ref(x, W_r, W_k, W_v, mu_r, mu_k):
        import jax, jax.numpy as jnp
        import numpy as np
        DIM = 128

        def _reference_tuple_inner(x, W_r, W_k, W_v, mu_r, mu_k):
            B, T, C = x.shape
            x_prev = jnp.concatenate([jnp.zeros((B, 1, C), x.dtype), x[:, :-1, :]], axis=1)
            xr = mu_r * x + (1.0 - mu_r) * x_prev
            xk = mu_k * x + (1.0 - mu_k) * x_prev
            r = jax.nn.sigmoid(jnp.einsum('btc,dc->btd', xr, W_r))
            k = jnp.einsum('btc,dc->btd', xk, W_k)
            k_act = jnp.square(jax.nn.relu(k))
            out = r * jnp.einsum('btc,dc->btd', k_act, W_v)
            new_state = x[:, -1, :]
            return (out, new_state)
        return _reference_tuple_inner(x, W_r, W_k, W_v, mu_r, mu_k)[0]
    x = L0_attn_x
    x = _layernorm(x + _L0_attn_ref(x, L0_attn_Wq, L0_attn_Wk, L0_attn_Wv, L0_attn_Wp, L0_attn_bp), axis=-1)
    x = _layernorm(x + _L0_ffn_ref(x, L0_ffn_W_r, L0_ffn_W_k, L0_ffn_W_v, L0_ffn_mu_r, L0_ffn_mu_k), axis=-1)
    return x

_drawn_inputs = setup_inputs


def setup_inputs(seed=0):
    import zlib

    import numpy as np

    out = dict(_drawn_inputs(seed))
    spreads = {'L0_attn_bp': (0.0, 0.1)}
    factors = {'L0_attn_Wq': 8.0,
     'L0_attn_Wk': 8.0,
     'L0_attn_Wv': 8.0,
     'L0_attn_Wp': 8.0,
     'L0_ffn_W_r': 3.154,
     'L0_ffn_mu_r': 6.231}
    for name, (base, spread) in spreads.items():
        noise = np.random.default_rng([zlib.crc32(name.encode()), seed]).standard_normal(out[name].shape)
        drawn = base * np.exp(spread * noise) if base else spread * noise
        out[name] = jnp.asarray(drawn.astype(out[name].dtype))
    for name, factor in factors.items():
        out[name] = (out[name] * factor).astype(out[name].dtype)
    return out
```

```python
import concourse.bass as bass
from concourse import mybir
from contextlib import ExitStack

F32 = mybir.dt.float32
ALU = mybir.AluOpType
ACT = mybir.ActivationFunctionType


def postln_block_kernel(nc, x, Wq, Wk, Wv, Wp, bp, W_r, W_k, W_v, mu_r, mu_k, out):
    B, T, E = x.shape
    H, D = 16, 8
    C = 32
    G = J = 4
    TT = T // E
    NB = E // C
    NCH = T // C
    V1 = D + 1
    GV = J * V1
    HV = H * V1
    LAST = 4
    DEN_EPS, LN_EPS = 1e-6, 1e-5
    DMA = 16
    assert E == 128 and H * D == E and T == TT * E and G * J == H

    with ExitStack() as ctx:
        def sb(name, shape):
            return ctx.enter_context(nc.sbuf_tensor(name, shape, F32))

        def ps(name, shape):
            return ctx.enter_context(nc.psum_tensor(name, shape, F32))

        def sem(name):
            return ctx.enter_context(nc.semaphore(name))

        ident = sb("ident", [E, E])
        causal = sb("causal", [E, C])
        head_of_group = sb("head_of_group", [E, J])
        state_mask = sb("state_mask", [E, GV])
        minus_half = sb("minus_half", [E, TT])
        bias_row = sb("bias_row", [E, E])
        mu = sb("mu", [E, 2])
        one_minus_mu = sb("one_minus_mu", [E, 2])
        w_in = sb("w_in", [E, 7, E])
        wp_in = sb("wp_in", [E, E])
        wT = sb("wT", [E, 7, E])
        WQ, WK, WV, WP, WR, WFK, WFV = range(7)

        x_sb = sb("x_sb", [E, 2, TT, E])
        xT = sb("xT", [E, T])
        e_z = sb("e_z", [E, 2, T])
        phiT = sb("phiT", [E, 2, 2, T])
        q_by_j = sb("q_by_j", [E, J, T])
        q_bd = sb("q_bd", [E, H, T])
        k_tok = sb("k_tok", [E, TT, E])
        v_bd = sb("v_bd", [E, 2, TT, NB, HV])
        A_sb = sb("A_sb", [E, 2, TT, H, C])
        sums = sb("sums", [E, TT, NB, GV])
        state = sb("state", [E, NCH + 1, GV])
        state_own = sb("state_own", [E, NCH, GV])
        state_bd = sb("state_bd", [E, G, NCH, GV])
        den = sb("den", [E, 2, C])
        rden = sb("rden", [E, 2, C])
        y = sb("y", [E, 2, 2 * E])
        yT = sb("yT", [E, T])
        xb = sb("xb", [E, 2, TT, E])
        z1 = sb("z1", [E, TT, E])
        stats1 = sb("stats1", [E, TT, 6])
        moments1 = sb("moments1", [E, 5, TT])
        var1 = sb("var1", [E, TT])
        rstd1 = sb("rstd1", [E, TT])
        shift1 = sb("shift1", [E, TT])
        x1 = sb("x1", [E, 2, TT, E])
        x1T = sb("x1T", [E, T + 1])
        mu_x = sb("mu_x", [E, 2, T])
        mixed = sb("mixed", [E, 2, T])
        th = sb("th", [E, TT, E])
        k_relu = sb("k_relu", [E, T])
        k_act = sb("k_act", [E, T])
        rk = sb("rk", [E, TT, E])
        z2 = sb("z2", [E, TT, E])
        stats2 = sb("stats2", [E, TT, 6])
        moments2 = sb("moments2", [E, 5, TT])
        var2 = sb("var2", [E, TT])
        rstd2 = sb("rstd2", [E, TT])
        shift2 = sb("shift2", [E, TT])
        o_sb = sb("o_sb", [E, 2, TT, E])

        pA = ps("pA", [E, 2, H, C])
        pZ = ps("pZ", [E, 2, T])
        pW = ps("pW", [E, 4, T])

        def tiles(bank):
            return pW[:, bank, :].rearrange("p (t f) -> p t f", t=TT)

        pXT, pV, pX1T, pR = pW[:, 0, :], tiles(0), pW[:, 0, :], tiles(0)
        pAV = [pW[:, 1 + k, 0:2 * HV].rearrange("p (t b n) -> p t b n", t=2, b=NB) for k in range(2)]
        pKV = pW[:, 2:4, 0:2 * HV].rearrange("p k (t b n) -> p k t b n", t=2, b=NB)
        pK, pF, pWP, pKT = pW[:, 3, :], tiles(3), tiles(1), tiles(2)

        CONSTS = 6 + 5 * (E // C)
        w_loaded, wp_permuted, pool_setup = sem("w_loaded"), sem("wp_permuted"), sem("pool_setup")
        w_ps, w_ready, dve_setup = sem("w_ps"), sem("w_ready"), sem("dve_setup")
        zeroed = sem("zeroed")
        x_in, out_done, q_bd_in, state_bd_in = sem("x_in"), sem("out_done"), sem("q_bd_in"), sem("state_bd_in")
        xT_ps, z_ps, v_ps, kT_ps, A_ps = sem("xT_ps"), sem("z_ps"), sem("v_ps"), sem("kT_ps"), sem("A_ps")
        av_ps, kv_ps, wp_ps, x1T_ps = sem("av_ps"), sem("kv_ps"), sem("wp_ps"), sem("x1T_ps")
        r_ps, k_ps, f_ps = sem("r_ps"), sem("k_ps"), sem("f_ps")
        xT_ready, e_ready, v_ready, q_by_j_ready = sem("xT_ready"), sem("e_ready"), sem("v_ready"), sem("q_by_j_ready")
        k_tok_ready, x1T_ready, th_ready = sem("k_tok_ready"), sem("x1T_ready"), sem("th_ready")
        relu_ready, o_ready = sem("relu_ready"), sem("o_ready")
        e_capped, phi_ready, A_masked, den_ready = sem("e_capped"), sem("phi_ready"), sem("A_masked"), sem("den_ready")
        rden_ready, y_ready, yT_ready, sum_ready = sem("rden_ready"), sem("y_ready"), sem("yT_ready"), sem("sum_ready")
        state_step, mixed_ready, z1_ready = sem("state_step"), sem("mixed_ready"), sem("z1_ready")
        stats1_ready, moments1_ready, var1_ready = sem("stats1_ready"), sem("moments1_ready"), sem("var1_ready")
        x1_ready, rk_ready, z2_ready = sem("x1_ready"), sem("rk_ready"), sem("z2_ready")
        stats2_ready, moments2_ready, var2_ready = sem("stats2_ready"), sem("moments2_ready"), sem("var2_ready")
        shift1_ready, shift2_ready = sem("shift1_ready"), sem("shift2_ready")
        xb_ready, state_own_ready, k_act_ready = sem("xb_ready"), sem("state_own_ready"), sem("k_act_ready")
        rstd1_ready, rstd2_ready = sem("rstd1_ready"), sem("rstd2_ready")

        def wait(eng, s, value):
            if not isinstance(value, int) or value > 0:
                eng.wait_ge(s, value)

        def held(eng, value):
            if not isinstance(value, int):
                eng.compute_val(value)
            return value

        FIRST_LOOPED = LAST + 1
        LOOP_END = B - 1
        assert (LOOP_END - FIRST_LOOPED) % 2 == 0

        def all_steps(eng, step):
            for i in range(FIRST_LOOPED):
                step(i, i % 2, lambda lag, i=i: 0 <= i - lag < B)
            with eng.Fori(0, (LOOP_END - FIRST_LOOPED) // 2) as pair:
                for k in range(2):
                    step(pair * 2 + (FIRST_LOOPED + k), (FIRST_LOOPED + k) % 2, lambda lag: True)
            for i in range(LOOP_END, B + LAST):
                step(i, i % 2, lambda lag, i=i: 0 <= i - lag < B)

        block = ctx.enter_context(nc.Block())

        @block.sync
        def _(sp):
            sp.dma_start(x_sb[:, 0, :, :], x[0, :, :].rearrange("(t p) f -> p t f", p=E)).then_inc(x_in, DMA)
            for k, w in enumerate((Wq, Wk, Wv, Wp, W_r, W_k, W_v)):
                sp.dma_start(w_in[:, k, :], w[:, :]).then_inc(w_loaded, DMA)
            sp.dma_start(bias_row[:, :], bp.rearrange("(a f) -> a f", a=1).broadcast_to([E, E])).then_inc(w_loaded, DMA)
            sp.dma_start(mu[:, 0:1], mu_r.rearrange("(f a) -> f a", a=1)).then_inc(w_loaded, DMA)
            sp.dma_start(mu[:, 1:2], mu_k.rearrange("(f a) -> f a", a=1)).then_inc(w_loaded, DMA)
            sp.wait_ge(zeroed, 3)

            def step(i, par, live):
                if live(-1):
                    n, used = held(sp, i + 1), held(sp, i)
                    held(sp, (i + 1) * (T * E) * 4)
                    wait(sp, xb_ready, used)
                    wait(sp, xT_ps, n)
                    sp.dma_start(x_sb[:, (par + 1) % 2, :, :],
                                 x[n, :, :].rearrange("(t p) f -> p t f", p=E)).then_inc(x_in, DMA)
                if live(4):
                    n, done, stored = held(sp, i - 4), held(sp, i - 3), held(sp, DMA * (i - 4))
                    held(sp, (i - 4) * (T * E) * 4)
                    wait(sp, out_done, stored)
                    sp.wait_ge(o_ready, done)
                    sp.dma_start(out[n, :, :].rearrange("(t p) f -> p t f", p=E),
                                 o_sb[:, par, :, :]).then_inc(out_done, DMA)
                if live(1):
                    n = i - 1
                    wait(sp, av_ps, 2 * n)
                    sp.wait_ge(state_own_ready, n + 1)
                    for g in range(G):
                        sp.dma_start(state_bd[C * g:C * g + C, g, :, :],
                                     state_own[C * g:C * g + C, :, :]).then_inc(state_bd_in, DMA)
                if live(0):
                    n = i
                    wait(sp, A_ps, TT * n)
                    sp.wait_ge(q_by_j_ready, n + 1)
                    for g in range(G):
                        sp.dma_start(q_bd[C * g:C * g + C, J * g:J * g + J, :],
                                     q_by_j[C * g:C * g + C, :, :]).then_inc(q_bd_in, DMA)

            all_steps(sp, step)
            sp.wait_ge(out_done, DMA * B)

        @block.gpsimd
        def _(pool):
            done = [0]

            def alone(ins):
                done[0] += 1
                ins.then_inc(pool_setup, 1)
                pool.wait_ge(pool_setup, done[0])

            def select(t, rows, compare, fill, base, pattern, step):
                alone(nc.gpsimd.affine_select(out=t[rows, :], in_=t[rows, :], compare_op=compare, fill=fill,
                                              base=base, pattern=pattern, channel_multiplier=step))

            alone(nc.gpsimd.memset(ident[:, :], 0.0))
            select(ident, slice(0, E), ALU.not_equal, 1.0, 0, [[-1, E]], 1)
            alone(nc.gpsimd.memset(causal[:, :], 1.0))
            alone(nc.gpsimd.memset(head_of_group[:, :], 1.0))
            alone(nc.gpsimd.memset(state_mask[:, :], 1.0))
            for q in range(E // C):
                rows = slice(C * q, C * q + C)
                select(causal, rows, ALU.is_ge, 0.0, 0, [[1, C]], -1)
                select(head_of_group, rows, ALU.is_ge, 0.0, 0, [[-D, J]], 1)
                select(head_of_group, rows, ALU.is_ge, 0.0, D - 1, [[D, J]], -1)
                select(state_mask, rows, ALU.is_ge, 0.0, 0, [[-D, J], [0, V1]], 1)
                select(state_mask, rows, ALU.is_ge, 0.0, D - 1, [[D, J], [0, V1]], -1)
            alone(nc.gpsimd.memset(minus_half[:, :], -0.5))
            nc.gpsimd.memset(q_bd[:, 0:H // 2, :], 0.0).then_inc(zeroed, 1)
            pool.wait_ge(w_loaded, 10 * DMA)

            def step(i, par, live):
                if live(1):
                    n, p = i - 1, (par - 1) % 2
                    pool.wait_ge(xT_ps, n + 1)
                    wait(pool, z1_ready, n - 1)
                    nc.gpsimd.tensor_tensor(xb[:, p, :, :], x_sb[:, p, :, :],
                                            bias_row[:, :].unsqueeze(1).broadcast_to([E, TT, E]),
                                            ALU.add).then_inc(xb_ready, 1)
                if live(1):
                    n = i - 1
                    pool.wait_ge(state_step, TT * (n + 1))
                    wait(pool, state_bd_in, G * DMA * n)
                    nc.gpsimd.tensor_tensor(state_own[:, :, :], state[:, 0:NCH, :],
                                            state_mask[:, :].unsqueeze(1).broadcast_to([E, NCH, GV]),
                                            ALU.mult).then_inc(state_own_ready, 1)
                if live(3):
                    n = i - 3
                    pool.wait_ge(relu_ready, n + 1)
                    wait(pool, f_ps, n)
                    nc.gpsimd.tensor_tensor(k_act[:, :], k_relu[:, :], k_relu[:, :], ALU.mult).then_inc(k_act_ready, 1)
                if live(3):
                    n = i - 3
                    pool.wait_ge(var2_ready, n + 1)
                    wait(pool, o_ready, n)
                    nc.gpsimd.tensor_tensor(rstd2[:, :], var2[:, :], minus_half[:, :], ALU.pow).then_inc(rstd2_ready, 1)
                if live(2):
                    n = i - 2
                    pool.wait_ge(var1_ready, n + 1)
                    wait(pool, x1_ready, n)
                    nc.gpsimd.tensor_tensor(rstd1[:, :], var1[:, :], minus_half[:, :], ALU.pow).then_inc(rstd1_ready, 1)

            all_steps(pool, step)

        @block.scalar
        def _(act):
            act.wait_ge(w_ps, 1)
            nc.scalar.activation(wT[:, 0:4, :], pA[:, 0, :, :].rearrange("p h c -> p (h c)").rearrange(
                "p (k f) -> p k f", k=4), ACT.Copy).then_inc(w_ready, 1)
            act.wait_ge(w_ps, 2)
            wB = pA[:, 1, :, :].rearrange("p h c -> p (h c)").rearrange("p (k f) -> p k f", k=4)
            nc.scalar.activation(wT[:, 4:6, :], wB[:, 0:2, :], ACT.Copy).then_inc(w_ready, 1)
            nc.scalar.activation(wT[:, 6, :], wB[:, 2, :], ACT.Copy, scale=0.5).then_inc(w_ready, 1)
            act.wait_ge(zeroed, 3)
            act.wait_ge(pool_setup, CONSTS)
            act.wait_ge(w_loaded, 10 * DMA)

            def step(i, par, live):
                if live(0):
                    n = i
                    act.wait_ge(xT_ps, n + 1)
                    wait(act, v_ps, n)
                    nc.scalar.activation(xT[:, :], pXT, ACT.Copy).then_inc(xT_ready, 1)
                if live(4):
                    n = i - 4
                    act.wait_ge(shift2_ready, n + 1)
                    wait(act, out_done, DMA * n)
                    for t in range(TT):
                        last = nc.scalar.activation(o_sb[:, par, t, :], z2[:, t, :], ACT.Identity,
                                                    bias=shift2[:, t:t + 1], scale=rstd2[:, t:t + 1])
                    last.then_inc(o_ready, 1)
                if live(3):
                    n = i - 3
                    act.wait_ge(x1T_ps, n + 1)
                    wait(act, mixed_ready, 2 * n)
                    nc.scalar.activation(x1T[:, 1:T + 1], pX1T, ACT.Copy)
                    for m in range(2):
                        last = nc.scalar.activation(mu_x[:, m, :], pX1T, ACT.Copy, scale=mu[:, m:m + 1])
                    last.then_inc(x1T_ready, 1)
                if live(3):
                    n = i - 3
                    act.wait_ge(r_ps, n + 1)
                    wait(act, rk_ready, n)
                    nc.scalar.activation(th[:, :, :], pR, ACT.Tanh, scale=0.5).then_inc(th_ready, 1)
                if live(0):
                    n = i
                    act.wait_ge(z_ps, n + 1)
                    wait(act, phi_ready, n)
                    nc.scalar.activation(e_z[:, :, :], pZ[:, :, :], ACT.Exp).then_inc(e_ready, 1)
                if live(3):
                    n = i - 3
                    act.wait_ge(k_ps, n + 1)
                    wait(act, k_act_ready, n)
                    nc.scalar.activation(k_relu[:, :], pK, ACT.Relu).then_inc(relu_ready, 1)
                if live(0):
                    n = i
                    act.wait_ge(v_ps, n + 1)
                    wait(act, av_ps, 2 * (n - 1))
                    for b in range(NB):
                        rows = slice(C * b, C * b + C)
                        last = nc.scalar.activation(
                            v_bd[rows, par, :, b, :].rearrange("p t (h e) -> p t h e", e=V1)[:, :, :, 0:D],
                            pV[rows, :, :].rearrange("p t (h e) -> p t h e", e=D), ACT.Copy)
                    last.then_inc(v_ready, 1)
                if live(0):
                    n = i
                    act.wait_ge(phi_ready, n + 1)
                    wait(act, q_bd_in, G * DMA * n)
                    for j in range(J):
                        last = nc.scalar.activation(q_by_j[:, j, :], phiT[:, par, 0, :], ACT.Copy,
                                                    scale=head_of_group[:, j:j + 1])
                    last.then_inc(q_by_j_ready, 1)
                if live(0):
                    n = i
                    act.wait_ge(kT_ps, n + 1)
                    wait(act, kv_ps, n)
                    nc.scalar.activation(k_tok[:, :, :], pKT, ACT.Copy).then_inc(k_tok_ready, 1)

            all_steps(act, step)

        @block.vector
        def _(dve):
            nc.vector.memset(q_bd[:, H // 2:H, :], 0.0).then_inc(zeroed, 1)
            nc.vector.memset(v_bd[:, :, :, :, :], 0.0).then_inc(dve_setup, 1)
            nc.vector.memset(state_bd[:, :, :, :], 0.0)
            nc.vector.memset(state[:, 0, :], 0.0)
            nc.vector.memset(x1T[:, 0:1], 0.0).then_inc(dve_setup, 1)
            dve.wait_ge(dve_setup, 2)
            for b in range(NB):
                for r in range(2):
                    last = nc.vector.memset(v_bd[C * b:C * b + C, r, :, b, :].rearrange(
                        "p t (h e) -> p t h e", e=V1)[:, :, :, D:V1], 1.0)
            last.then_inc(zeroed, 1)
            dve.wait_ge(w_loaded, 10 * DMA)
            nc.vector.tensor_copy(wp_in[:, :].rearrange("p (j g e) -> p j g e", j=J, g=G),
                                  w_in[:, WP, :].rearrange("p (g j e) -> p j g e", g=G, j=J)).then_inc(wp_permuted, 1)
            nc.vector.tensor_scalar(one_minus_mu[:, :], mu[:, :], -1.0, 1.0, ALU.mult, ALU.add).then_inc(dve_setup, 1)
            dve.wait_ge(dve_setup, 3)
            dve.wait_ge(pool_setup, CONSTS)

            def normalize_attention(i, par, pair):
                n = i - 2
                k = 2 * n + pair
                dve.wait_ge(av_ps, k + 1)
                flat = pAV[pair].rearrange("p t b (g e) -> p (t b g) e", e=V1)
                nc.vector.tensor_scalar(den[:, pair, :], flat[:, :, D], DEN_EPS, None, ALU.add).then_inc(den_ready, 1)
                dve.wait_ge(den_ready, k + 1)
                nc.vector.reciprocal(rden[:, pair, :], den[:, pair, :]).then_inc(rden_ready, 1)
                dve.wait_ge(rden_ready, k + 1)
                nc.vector.tensor_tensor(y[:, pair, :].rearrange("p (a e) -> p a e", e=D), flat[:, :, 0:D],
                                        rden[:, pair, :].unsqueeze(2).broadcast_to([E, C, D]),
                                        ALU.mult).then_inc(y_ready, 1)
                dve.wait_ge(y_ready, k + 1)
                wait(dve, wp_ps, n)
                nc.vector.transpose(yT[:, 2 * E * pair:2 * E * (pair + 1)], y[:, pair, :]).then_inc(yT_ready, 1)

            def mask_scores(i, par, t):
                n, p = i - 1, (par - 1) % 2
                dve.wait_ge(A_ps, TT * n + t + 1)
                wait(dve, av_ps, 2 * (n - 2) + t // 2 + 1)
                nc.vector.tensor_tensor(A_sb[:, p, t, :, :], pA[:, t % 2, :, :],
                                        causal[:, :].unsqueeze(1).broadcast_to([E, H, C]),
                                        ALU.mult).then_inc(A_masked, 1)

            def variance(n, z, stats, moments, var, stats_ready, moments_ready, var_ready):
                twice_mean, diff, cv, diff2, within = (moments[:, k, :] for k in range(5))
                for t in range(TT):
                    nc.vector.bn_stats(stats[:, t, :], z[:, t, :]).then_inc(stats_ready, 1)
                dve.wait_ge(stats_ready, TT * (n + 1))
                nc.vector.tensor_tensor(diff, stats[:, :, 1], stats[:, :, 4], ALU.subtract).then_inc(moments_ready, 1)
                nc.vector.tensor_tensor(cv, stats[:, :, 2], stats[:, :, 5], ALU.add).then_inc(moments_ready, 1)
                nc.vector.tensor_tensor(twice_mean, stats[:, :, 1], stats[:, :, 4], ALU.add).then_inc(moments_ready, 1)
                dve.wait_ge(moments_ready, 5 * n + 3)
                nc.vector.scalar_tensor_tensor(diff2, diff, 0.25, diff, ALU.mult, ALU.mult).then_inc(moments_ready, 1)
                nc.vector.tensor_scalar(within, cv, 1.0 / E, LN_EPS, ALU.mult, ALU.add).then_inc(moments_ready, 1)
                dve.wait_ge(moments_ready, 5 * (n + 1))
                nc.vector.tensor_tensor(var[:, :], diff2, within, ALU.add).then_inc(var_ready, 1)

            def step(i, par, live):
                if live(4):
                    n = i - 4
                    dve.wait_ge(rstd2_ready, n + 1)
                    nc.vector.scalar_tensor_tensor(shift2[:, :], moments2[:, 0, :], -0.5, rstd2[:, :],
                                                   ALU.mult, ALU.mult).then_inc(shift2_ready, 1)
                if live(2):
                    normalize_attention(i, par, 0)
                if live(1):
                    n = i - 1
                    dve.wait_ge(kv_ps, n + 1)
                    kv = pKV
                    s4 = sums[:, :, :, :].rearrange("p (k t) b n -> p k t b n", k=2)
                    nc.vector.tensor_copy(s4[:, :, :, 0, :], kv[:, :, :, 0, :]).then_inc(sum_ready, 1)
                    for b in range(1, NB):
                        dve.wait_ge(sum_ready, NB * n + b)
                        nc.vector.tensor_tensor(s4[:, :, :, b, :], kv[:, :, :, b, :], s4[:, :, :, b - 1, :],
                                                ALU.add).then_inc(sum_ready, 1)
                    dve.wait_ge(sum_ready, NB * (n + 1))
                    wait(dve, state_own_ready, n)
                    for t in range(TT):
                        if t:
                            dve.wait_ge(state_step, TT * n + t)
                        nc.vector.tensor_tensor(state[:, NB * t + 1:NB * t + 1 + NB, :], sums[:, t, :, :],
                                                state[:, NB * t:NB * t + 1, :].broadcast_to([E, NB, GV]),
                                                ALU.add).then_inc(state_step, 1)
                if live(1):
                    mask_scores(i, par, 0)
                    mask_scores(i, par, 1)
                if live(3):
                    n = i - 3
                    dve.wait_ge(x1T_ready, n + 1)
                    wait(dve, k_ps, n)
                    for m in range(2):
                        nc.vector.scalar_tensor_tensor(mixed[:, m, :], x1T[:, 0:T], one_minus_mu[:, m:m + 1],
                                                       mu_x[:, m, :], ALU.mult, ALU.add).then_inc(mixed_ready, 1)
                if live(2):
                    normalize_attention(i, par, 1)
                if live(0):
                    n = i
                    dve.wait_ge(e_ready, n + 1)
                    nc.vector.tensor_scalar(e_z[:, :, :], e_z[:, :, :], 1.0, None, ALU.min).then_inc(e_capped, 1)
                    dve.wait_ge(e_capped, n + 1)
                    wait(dve, av_ps, 2 * (n - 1))
                    nc.vector.scalar_tensor_tensor(phiT[:, par, :, :], pZ[:, :, :], 0.0, e_z[:, :, :],
                                                   ALU.max, ALU.add).then_inc(phi_ready, 1)
                if live(1):
                    mask_scores(i, par, 2)
                if live(3):
                    n, p = i - 3, (par - 3) % 2
                    dve.wait_ge(th_ready, n + 1)
                    dve.wait_ge(f_ps, n + 1)
                    nc.vector.scalar_tensor_tensor(rk[:, :, :], th[:, :, :], 1.0, pF, ALU.add,
                                                   ALU.mult).then_inc(rk_ready, 1)
                    dve.wait_ge(rk_ready, n + 1)
                    wait(dve, o_ready, n)
                    nc.vector.tensor_tensor(z2[:, :, :], rk[:, :, :], x1[:, p, :, :], ALU.add).then_inc(z2_ready, 1)
                    dve.wait_ge(z2_ready, n + 1)
                    variance(n, z2, stats2, moments2, var2, stats2_ready, moments2_ready, var2_ready)
                if live(2):
                    n, p = i - 2, par
                    dve.wait_ge(wp_ps, n + 1)
                    dve.wait_ge(xb_ready, n + 1)
                    nc.vector.tensor_tensor(z1[:, :, :], pWP, xb[:, p, :, :], ALU.add).then_inc(z1_ready, 1)
                    dve.wait_ge(z1_ready, n + 1)
                    variance(n, z1, stats1, moments1, var1, stats1_ready, moments1_ready, var1_ready)
                if live(1):
                    mask_scores(i, par, 3)
                if live(2):
                    n, p = i - 2, par
                    dve.wait_ge(rstd1_ready, n + 1)
                    nc.vector.scalar_tensor_tensor(shift1[:, :], moments1[:, 0, :], -0.5, rstd1[:, :],
                                                   ALU.mult, ALU.mult).then_inc(shift1_ready, 1)
                    dve.wait_ge(shift1_ready, n + 1)
                    wait(dve, x1T_ps, n - 1)
                    for t in range(TT):
                        last = nc.vector.tensor_scalar(x1[:, p, t, :], z1[:, t, :], rstd1[:, t:t + 1],
                                                       shift1[:, t:t + 1], ALU.mult, ALU.add)
                    last.then_inc(x1_ready, 1)

            all_steps(dve, step)

        @block.tensor
        def _(pe):
            mm = nc.tensor.matmul
            pe.wait_ge(pool_setup, 2)
            pe.wait_ge(w_loaded, 10 * DMA)
            pe.wait_ge(wp_permuted, 1)
            for half, ws in enumerate(((WQ, WK, WV, WP), (WR, WFK, WFV))):
                dst = pA[:, half, :, :].rearrange("p h c -> p (h c)")
                for k, w in enumerate(ws):
                    src = wp_in[:, :] if w == WP else w_in[:, w, :]
                    last = nc.tensor.transpose(dst[:, E * k:E * (k + 1)], src, ident[:, :])
                last.then_inc(w_ps, 1)
            pe.wait_ge(w_ready, 3)

            def scores(i, par, t):
                n, p = i - 1, (par - 1) % 2
                k = TT * n + t
                if t == 0:
                    pe.wait_ge(q_bd_in, G * DMA * (n + 1))
                wait(pe, A_masked, k - 1)
                for b in range(NB):
                    tok = E * t + C * b
                    last = mm(pA[C * b:C * b + C, t % 2, :, :], phiT[:, p, 1, tok:tok + C],
                              q_bd[:, :, tok:tok + C], start=True, stop=True)
                last.then_inc(A_ps, 1)

            def attend(i, par, pair):
                n, p = i - 2, par
                for t2 in range(2):
                    t = 2 * pair + t2
                    for g in range(G):
                        for j in range(J):
                            h = J * g + j
                            mm(pAV[pair][C * j:C * j + C, t2, :, V1 * g:V1 * g + V1], A_sb[:, p, t, h, :],
                               v_bd[:, p, t, :, V1 * h:V1 * h + V1], start=(t2 == 0 and g == 0), stop=False,
                               skip_group_check=True)
                if pair == 0:
                    pe.wait_ge(state_bd_in, G * DMA * (n + 1))
                for t2 in range(2):
                    for b in range(NB):
                        ch = NB * (2 * pair + t2) + b
                        if ch == 0:
                            continue
                        for j in range(J):
                            last = mm(pAV[pair][C * j:C * j + C, t2, b, :], phiT[:, p, 0, C * ch:C * ch + C],
                                      state_bd[:, :, ch, V1 * j:V1 * j + V1], start=False,
                                      stop=(t2 == 1 and b == NB - 1), skip_group_check=True)
                last.then_inc(av_ps, 1)

            def step(i, par, live):
                if live(0):
                    n = i
                    pe.wait_ge(x_in, DMA * (n + 1))
                    wait(pe, v_ready, n)
                    for t in range(TT):
                        last = nc.tensor.transpose(pXT[:, E * t:E * t + E], x_sb[:, par, t, :], ident[:, :])
                    last.then_inc(xT_ps, 1)
                if live(2):
                    n = i - 2
                    wait(pe, z1_ready, n)
                    pe.wait_ge(A_masked, TT * n + 2)
                    attend(i, par, 0)
                if live(1):
                    n, p = i - 1, (par - 1) % 2
                    pe.wait_ge(k_tok_ready, n + 1)
                    pe.wait_ge(v_ready, n + 1)
                    wait(pe, rk_ready, n - 2)
                    for t in range(TT):
                        for g in range(G):
                            last = mm(pKV[C * g:C * g + C, t // 2, t % 2, :, :], k_tok[:, t, C * g:C * g + C],
                                      v_bd[:, p, t, :, GV * g:GV * g + GV], start=True, stop=True)
                    last.then_inc(kv_ps, 1)
                if live(3):
                    n, p = i - 3, (par - 3) % 2
                    pe.wait_ge(x1_ready, n + 1)
                    if live(0):
                        pe.wait_ge(xT_ready, i + 1)
                    else:
                        pe.wait_ge(v_ready, B)
                    for t in range(TT):
                        last = nc.tensor.transpose(pX1T[:, E * t:E * t + E], x1[:, p, t, :], ident[:, :])
                    last.then_inc(x1T_ps, 1)
                if live(1):
                    scores(i, par, 0)
                    scores(i, par, 1)
                if live(2):
                    n = i - 2
                    if live(1):
                        pe.wait_ge(sum_ready, NB * i)
                    pe.wait_ge(A_masked, TT * n + 4)
                    attend(i, par, 1)
                if live(3):
                    n = i - 3
                    pe.wait_ge(mixed_ready, 2 * n + 1)
                    for t in range(TT):
                        last = mm(pR[:, t, :], mixed[:, 0, E * t:E * t + E], wT[:, WR, :], start=True, stop=True)
                    last.then_inc(r_ps, 1)
                if live(0):
                    n = i
                    pe.wait_ge(xT_ready, n + 1)
                    wait(pe, phi_ready, n)
                    mm(pZ[:, 0, :], wT[:, WQ, :], xT[:, :], start=True, stop=True)
                    mm(pZ[:, 1, :], wT[:, WK, :], xT[:, :], start=True, stop=True).then_inc(z_ps, 1)
                if live(3):
                    n = i - 3
                    pe.wait_ge(mixed_ready, 2 * n + 2)
                    if live(1):
                        pe.wait_ge(sum_ready, NB * i)
                    else:
                        pe.wait_ge(rk_ready, n)
                    mm(pK, wT[:, WFK, :], mixed[:, 1, :], start=True, stop=True).then_inc(k_ps, 1)
                if live(0):
                    n = i
                    if live(3):
                        pe.wait_ge(th_ready, n - 2)
                    for t in range(TT):
                        last = mm(pV[:, t, :], xT[:, E * t:E * t + E], wT[:, WV, :], start=True, stop=True)
                    last.then_inc(v_ps, 1)
                if live(1):
                    scores(i, par, 2)
                if live(3):
                    n = i - 3
                    pe.wait_ge(k_act_ready, n + 1)
                    for t in range(TT):
                        last = mm(pF[:, t, :], k_act[:, E * t:E * t + E], wT[:, WFV, :], start=True, stop=True)
                    last.then_inc(f_ps, 1)
                if live(2):
                    n = i - 2
                    pe.wait_ge(yT_ready, 2 * (n + 1))
                    for t in range(TT):
                        last = mm(pWP[:, t, :], yT[:, E * t:E * t + E], wT[:, WP, :], start=True, stop=True)
                    last.then_inc(wp_ps, 1)
                if live(1):
                    scores(i, par, 3)
                if live(0):
                    n = i
                    pe.wait_ge(phi_ready, n + 1)
                    wait(pe, y_ready, 2 * (n - 1))
                    if not live(2) and live(1):
                        pe.wait_ge(sum_ready, NB * n)
                    for t in range(TT):
                        last = nc.tensor.transpose(pKT[:, t, :], phiT[:, par, 1, E * t:E * t + E], ident[:, :])
                    last.then_inc(kT_ps, 1)

            all_steps(pe, step)


_INS = ["L0_attn_x", "L0_attn_Wq", "L0_attn_Wk", "L0_attn_Wv", "L0_attn_Wp", "L0_attn_bp",
        "L0_ffn_W_r", "L0_ffn_W_k", "L0_ffn_W_v", "L0_ffn_mu_r", "L0_ffn_mu_k"]


def kernel(**inputs):
    import numpy as _np
    import concourse.bacc as _bacc
    from concourse import mybir as _mybir
    from concourse.bass_utils import run_bass_kernel_spmd as _run

    nc = _bacc.Bacc("TRN2", target_bir_lowering=False, num_devices=1)
    arrays, args = {}, []
    for name in _INS:
        a = _np.ascontiguousarray(inputs[name])
        arrays[f"in_{name}"] = a
        args.append(nc.dram_tensor(f"in_{name}", a.shape, _mybir.dt.from_np(a.dtype), kind="ExternalInput").ap())
    shape = arrays["in_L0_attn_x"].shape
    args.append(nc.dram_tensor("out_0", shape, _mybir.dt.float32, kind="ExternalOutput").ap())
    postln_block_kernel(nc, *args)
    r = _run(nc, [arrays], core_ids=[0])
    return r.results[0]["out_0"]
```

```python
import concourse.bass as bass
from concourse import mybir
from contextlib import ExitStack

F32 = mybir.dt.float32
ALU = mybir.AluOpType
ACT = mybir.ActivationFunctionType


def postln_block_kernel(nc, x, Wq, Wk, Wv, Wp, bp, W_r, W_k, W_v, mu_r, mu_k, out):
    B, T, E = x.shape
    H, D = 16, 8
    C = 32
    G = J = 4
    TT = T // E
    NB = E // C
    NCH = T // C
    V1 = D + 1
    GV = J * V1
    HV = H * V1
    LAST = 4
    DEN_EPS, LN_EPS = 1e-6, 1e-5
    DMA = 16
    assert E == 128 and H * D == E and T == TT * E and G * J == H

    with ExitStack() as ctx:
        def sb(name, shape):
            return ctx.enter_context(nc.sbuf_tensor(name, shape, F32))

        def ps(name, shape):
            return ctx.enter_context(nc.psum_tensor(name, shape, F32))

        def sem(name):
            return ctx.enter_context(nc.semaphore(name))

        ident = sb("ident", [E, E])
        causal = sb("causal", [E, C])
        head_of_group = sb("head_of_group", [E, J])
        state_mask = sb("state_mask", [E, GV])
        restart = sb("restart", [E, GV // 2, NCH])
        minus_half = sb("minus_half", [E, 2 * TT])
        bias_row = sb("bias_row", [E, E])
        mu = sb("mu", [E, 2])
        one_minus_mu = sb("one_minus_mu", [E, 2])
        w_in = sb("w_in", [E, 7, E])
        wp_in = sb("wp_in", [E, E])
        wT = sb("wT", [E, 7, E])
        WQ, WK, WV, WP, WR, WFK, WFV = range(7)

        x_sb = sb("x_sb", [E, 2, TT, E])
        xT = sb("xT", [E, T])
        e_z = sb("e_z", [E, 2, T])
        r_z = sb("r_z", [E, 2, T])
        phiT = sb("phiT", [E, 2, 2, T])
        q_by_j = sb("q_by_j", [E, J, T])
        q_bd = sb("q_bd", [E, H, T])
        k_tok = sb("k_tok", [E, TT, E])
        v_bd = sb("v_bd", [E, 2, TT, NB, HV])
        A_sb = sb("A_sb", [E, TT, H, C])
        state = sb("state", [E, 1 + GV * NCH])
        state_own = sb("state_own", [E, NCH - 1, GV])
        state_bd = sb("state_bd", [E, G, NCH - 1, GV])
        den = sb("den", [E, 2 * C])
        rden = sb("rden", [E, 2 * C])
        y = sb("y", [E, T])
        yT = sb("yT", [E, T])
        xb = sb("xb", [E, 2, TT, E])
        z1 = sb("z1", [E, TT, E])
        x1 = sb("x1", [E, 2, TT, E])
        x1T = sb("x1T", [E, T + 1])
        mu_x = sb("mu_x", [E, 2, T])
        mixed = sb("mixed", [E, 2, T])
        th = sb("th", [E, TT, E])
        k_relu = sb("k_relu", [E, T])
        k_act = sb("k_act", [E, T])
        rk = sb("rk", [E, TT, E])
        z2 = sb("z2", [E, TT, E])
        stats = sb("stats", [E, 2 * TT, 6])
        moments = sb("moments", [E, 5, 2 * TT])
        var = sb("var", [E, 2 * TT])
        rstd = sb("rstd", [E, 2 * TT])
        shift = sb("shift", [E, 2 * TT])
        o_sb = sb("o_sb", [E, 2, TT, E])

        pA = ps("pA", [E, 2, H, C])
        pZ = ps("pZ", [E, 2, T])
        pW = ps("pW", [E, 4, T])

        def tiles(bank):
            return pW[:, bank, :].rearrange("p (t f) -> p t f", t=TT)

        pXT, pX1T, pKT, pV, pWP, pF = pW[:, 0, :], pW[:, 0, :], tiles(0), tiles(1), tiles(2), tiles(3)
        pR, pK = pZ[:, 0, :].rearrange("p (t f) -> p t f", t=TT), pZ[:, 1, :]
        pAV = pW[:, 1:3, 0:2 * HV].rearrange("p k (t b n) -> p k t b n", t=2, b=NB)
        KVH = GV // 2 * NCH
        pKV = pZ[:, :, 0:KVH].rearrange("p k (n t b) -> p k t b n", t=TT, b=NB)

        CONSTS = 8 + 5 * (E // C)
        qkv_loaded, w_loaded, wp_permuted, pool_setup = sem("qkv_loaded"), sem("w_loaded"), sem("wp_permuted"), sem("pool_setup")
        w_ps, w_ready, dve_setup = sem("w_ps"), sem("w_ready"), sem("dve_setup")
        v_bd_zeroed, q_bd_zeroed, state_bd_zeroed = sem("v_bd_zeroed"), sem("q_bd_zeroed"), sem("state_bd_zeroed")
        x_in, out_done, q_bd_in, state_bd_in = sem("x_in"), sem("out_done"), sem("q_bd_in"), sem("state_bd_in")
        xT_ps, z_ps, v_ps, kT_ps, A_ps = sem("xT_ps"), sem("z_ps"), sem("v_ps"), sem("kT_ps"), sem("A_ps")
        av_ps, kv_ps, wp_ps, x1T_ps = sem("av_ps"), sem("kv_ps"), sem("wp_ps"), sem("x1T_ps")
        r_ps, k_ps, f_ps = sem("r_ps"), sem("k_ps"), sem("f_ps")
        xT_ready, z_read, v_ready, q_by_j_ready = sem("xT_ready"), sem("z_read"), sem("v_ready"), sem("q_by_j_ready")
        k_tok_ready, x1T_ready, th_ready = sem("k_tok_ready"), sem("x1T_ready"), sem("th_ready")
        relu_ready, o_ready = sem("relu_ready"), sem("o_ready")
        phi_ready, A_masked, den_ready = sem("phi_ready"), sem("A_masked"), sem("den_ready")
        rden_ready, y_ready, yT_ready, state_ready = sem("rden_ready"), sem("y_ready"), sem("yT_ready"), sem("state_ready")
        mixed_ready, z1_ready = sem("mixed_ready"), sem("z1_ready")
        stats1_ready, stats2_ready = sem("stats1_ready"), sem("stats2_ready")
        moments_ready, var_ready, shift_ready = sem("moments_ready"), sem("var_ready"), sem("shift_ready")
        x1_ready, rk_ready = sem("x1_ready"), sem("rk_ready")
        xb_ready, state_own_ready, k_act_ready = sem("xb_ready"), sem("state_own_ready"), sem("k_act_ready")
        z2_ready, rstd_ready = sem("z2_ready"), sem("rstd_ready")

        def wait(eng, s, value):
            if not isinstance(value, int) or value > 0:
                eng.wait_ge(s, value)

        def held(eng, value):
            if not isinstance(value, int):
                eng.compute_val(value)
            return value

        def norm_columns(live):
            return slice(0 if live(3) else TT, 2 * TT if live(4) else TT)

        FIRST_LOOPED = LAST + 1
        LOOP_END = B - 1
        assert (LOOP_END - FIRST_LOOPED) % 2 == 0

        def all_steps(eng, step):
            for i in range(FIRST_LOOPED):
                step(i, i % 2, lambda lag, i=i: 0 <= i - lag < B)
            with eng.Fori(0, (LOOP_END - FIRST_LOOPED) // 2) as pair:
                for k in range(2):
                    step(pair * 2 + (FIRST_LOOPED + k), (FIRST_LOOPED + k) % 2, lambda lag: True)
            for i in range(LOOP_END, B + LAST):
                step(i, i % 2, lambda lag, i=i: 0 <= i - lag < B)

        block = ctx.enter_context(nc.Block())

        @block.sync
        def _(sp):
            weights = tuple(enumerate((Wq, Wk, Wv, Wp, W_r, W_k, W_v)))
            sp.dma_start(x_sb[:, 0, :, :], x[0, :, :].rearrange("(t p) f -> p t f", p=E)).then_inc(x_in, DMA)
            for k, w in weights[:3]:
                sp.dma_start(w_in[:, k, :], w[:, :]).then_inc(qkv_loaded, DMA)
            for k, w in weights[3:]:
                sp.dma_start(w_in[:, k, :], w[:, :]).then_inc(w_loaded, DMA)
            sp.dma_start(bias_row[:, :], bp.rearrange("(a f) -> a f", a=1).broadcast_to([E, E])).then_inc(w_loaded, DMA)
            sp.dma_start(mu[:, 0:1], mu_r.rearrange("(f a) -> f a", a=1)).then_inc(w_loaded, DMA)
            sp.dma_start(mu[:, 1:2], mu_k.rearrange("(f a) -> f a", a=1)).then_inc(w_loaded, DMA)

            def step(i, par, live):
                if live(1):
                    n, own = held(sp, i - 1), held(sp, i)
                    if not live(2):
                        sp.wait_ge(state_bd_zeroed, 1)
                    wait(sp, av_ps, n)
                    sp.wait_ge(state_own_ready, own)
                    for g in range(G):
                        sp.dma_start(state_bd[C * g:C * g + C, g, :, :],
                                     state_own[C * g:C * g + C, :, :]).then_inc(state_bd_in, DMA)
                if live(4):
                    n, done, stored = held(sp, i - 4), held(sp, i - 3), held(sp, DMA * (i - 4))
                    held(sp, (i - 4) * (T * E) * 4)
                    wait(sp, out_done, stored)
                    sp.wait_ge(o_ready, done)
                    sp.dma_start(out[n, :, :].rearrange("(t p) f -> p t f", p=E),
                                 o_sb[:, par, :, :]).then_inc(out_done, DMA)
                if live(-1):
                    n, used = held(sp, i + 1), held(sp, i)
                    held(sp, (i + 1) * (T * E) * 4)
                    wait(sp, xb_ready, used)
                    wait(sp, xT_ps, n)
                    sp.dma_start(x_sb[:, (par + 1) % 2, :, :],
                                 x[n, :, :].rearrange("(t p) f -> p t f", p=E)).then_inc(x_in, DMA)
                if live(0):
                    used, ready = held(sp, TT * i), held(sp, i + 1)
                    if not live(1):
                        sp.wait_ge(q_bd_zeroed, 2)
                    wait(sp, A_ps, used)
                    sp.wait_ge(q_by_j_ready, ready)
                    for g in range(G):
                        sp.dma_start(q_bd[C * g:C * g + C, J * g:J * g + J, :],
                                     q_by_j[C * g:C * g + C, :, :]).then_inc(q_bd_in, DMA)

            all_steps(sp, step)
            sp.wait_ge(out_done, DMA * B)

        @block.gpsimd
        def _(pool):
            done = [0]

            def alone(ins):
                done[0] += 1
                ins.then_inc(pool_setup, 1)
                pool.wait_ge(pool_setup, done[0])

            def select(t, rows, compare, fill, base, pattern, step):
                alone(nc.gpsimd.affine_select(out=t[rows, :], in_=t[rows, :], compare_op=compare, fill=fill,
                                              base=base, pattern=pattern, channel_multiplier=step))

            alone(nc.gpsimd.memset(ident[:, :], 0.0))
            select(ident, slice(0, E), ALU.not_equal, 1.0, 0, [[-1, E]], 1)
            alone(nc.gpsimd.memset(causal[:, :], 1.0))
            alone(nc.gpsimd.memset(head_of_group[:, :], 1.0))
            alone(nc.gpsimd.memset(state_mask[:, :], 1.0))
            for q in range(E // C):
                rows = slice(C * q, C * q + C)
                select(causal, rows, ALU.is_ge, 0.0, 0, [[1, C]], -1)
                select(head_of_group, rows, ALU.is_ge, 0.0, 0, [[-D, J]], 1)
                select(head_of_group, rows, ALU.is_ge, 0.0, D - 1, [[D, J]], -1)
                select(state_mask, rows, ALU.is_ge, 0.0, 0, [[-D, J], [0, V1]], 1)
                select(state_mask, rows, ALU.is_ge, 0.0, D - 1, [[D, J], [0, V1]], -1)
            alone(nc.gpsimd.memset(minus_half[:, :], -0.5))
            alone(nc.gpsimd.memset(restart[:, :, :], 1.0))
            alone(nc.gpsimd.memset(restart[:, :, 0:1], 0.0))
            nc.gpsimd.memset(q_bd[:, 0:H // 2, :], 0.0).then_inc(q_bd_zeroed, 1)

            def step(i, par, live):
                if live(4):
                    n, p = i - 4, par
                    pool.wait_ge(rk_ready, n + 1)
                    wait(pool, o_ready, n)
                    nc.gpsimd.tensor_tensor(z2[:, :, :], rk[:, :, :], x1[:, p, :, :], ALU.add).then_inc(z2_ready, 1)
                if live(3) or live(4):
                    m, cols = i - 3, norm_columns(live)
                    pool.wait_ge(var_ready, m + 1)
                    wait(pool, x1_ready, m)
                    wait(pool, o_ready, m - 1)
                    nc.gpsimd.tensor_tensor(rstd[:, cols], var[:, cols], minus_half[:, cols],
                                            ALU.pow).then_inc(rstd_ready, 1)
                if live(1):
                    n = i - 1
                    pool.wait_ge(state_ready, 2 * (n + 1))
                    wait(pool, state_bd_in, G * DMA * n)
                    nc.gpsimd.tensor_tensor(state_own[:, :, :],
                                            state[:, 0:GV * NCH].rearrange("p (n c) -> p c n", c=NCH)[:, 1:NCH, :],
                                            state_mask[:, :].unsqueeze(1).broadcast_to([E, NCH - 1, GV]),
                                            ALU.mult).then_inc(state_own_ready, 1)
                if live(1):
                    n, p = i - 1, (par - 1) % 2
                    if not live(2):
                        pool.wait_ge(w_loaded, 7 * DMA)
                    pool.wait_ge(xT_ps, n + 1)
                    wait(pool, z1_ready, n - 1)
                    nc.gpsimd.tensor_tensor(xb[:, p, :, :], x_sb[:, p, :, :],
                                            bias_row[:, :].unsqueeze(1).broadcast_to([E, TT, E]),
                                            ALU.add).then_inc(xb_ready, 1)
                if live(3):
                    n = i - 3
                    pool.wait_ge(relu_ready, n + 1)
                    wait(pool, f_ps, n)
                    nc.gpsimd.tensor_tensor(k_act[:, :], k_relu[:, :], k_relu[:, :], ALU.mult).then_inc(k_act_ready, 1)

            all_steps(pool, step)

        @block.scalar
        def _(act):
            wA, wB = (pA[:, half, :, :].rearrange("p h c -> p (h c)").rearrange("p (k f) -> p k f", k=4)
                      for half in range(2))
            act.wait_ge(w_ps, 1)
            nc.scalar.activation(wT[:, 0:3, :], wA[:, 0:3, :], ACT.Copy).then_inc(w_ready, 1)
            act.wait_ge(w_ps, 2)
            nc.scalar.activation(wT[:, 3:6, :], wB[:, 0:3, :], ACT.Copy).then_inc(w_ready, 1)
            nc.scalar.activation(wT[:, 6, :], wB[:, 3, :], ACT.Copy, scale=0.5).then_inc(w_ready, 1)
            act.wait_ge(pool_setup, CONSTS)

            def step(i, par, live):
                if live(0):
                    n = i
                    act.wait_ge(xT_ps, n + 1)
                    wait(act, v_ps, n)
                    nc.scalar.activation(xT[:, :], pXT, ACT.Copy).then_inc(xT_ready, 1)
                if live(4):
                    n = i - 4
                    act.wait_ge(shift_ready, n + 2)
                    wait(act, out_done, DMA * n)
                    for t in range(TT):
                        last = nc.scalar.activation(o_sb[:, par, t, :], z2[:, t, :], ACT.Identity,
                                                    bias=shift[:, TT + t:TT + t + 1], scale=rstd[:, TT + t:TT + t + 1])
                    last.then_inc(o_ready, 1)
                if live(3):
                    n = i - 3
                    act.wait_ge(x1T_ps, n + 1)
                    if not live(4):
                        act.wait_ge(w_loaded, 7 * DMA)
                    wait(act, mixed_ready, 2 * n)
                    nc.scalar.activation(x1T[:, 1:T + 1], pX1T, ACT.Copy)
                    for m in range(2):
                        last = nc.scalar.activation(mu_x[:, m, :], pX1T, ACT.Copy, scale=mu[:, m:m + 1])
                    last.then_inc(x1T_ready, 1)
                if live(0):
                    n = i
                    act.wait_ge(z_ps, n + 1)
                    wait(act, phi_ready, n)
                    nc.scalar.activation(e_z[:, :, :], pZ[:, :, :], ACT.Exp)
                    nc.scalar.activation(r_z[:, :, :], pZ[:, :, :], ACT.Relu).then_inc(z_read, 1)
                if live(0):
                    n = i
                    if not live(1):
                        act.wait_ge(v_bd_zeroed, 1)
                    act.wait_ge(v_ps, n + 1)
                    wait(act, av_ps, n - 1)
                    for b in range(NB):
                        rows = slice(C * b, C * b + C)
                        last = nc.scalar.activation(
                            v_bd[rows, par, :, b, :].rearrange("p t (h e) -> p t h e", e=V1)[:, :, :, 0:D],
                            pV[rows, :, :].rearrange("p t (h e) -> p t h e", e=D), ACT.Copy)
                    last.then_inc(v_ready, 1)
                if live(3):
                    n = i - 3
                    act.wait_ge(k_ps, n + 1)
                    wait(act, k_act_ready, n)
                    nc.scalar.activation(k_relu[:, :], pK, ACT.Relu).then_inc(relu_ready, 1)
                if live(3):
                    n = i - 3
                    wait(act, rk_ready, n)
                    act.wait_ge(r_ps, n + 1)
                    nc.scalar.activation(th[:, :, :], pR, ACT.Tanh, scale=0.5).then_inc(th_ready, 1)
                if live(0):
                    n = i
                    act.wait_ge(phi_ready, n + 1)
                    wait(act, q_bd_in, G * DMA * n)
                    for j in range(J):
                        last = nc.scalar.activation(q_by_j[:, j, :], phiT[:, par, 0, :], ACT.Copy,
                                                    scale=head_of_group[:, j:j + 1])
                    last.then_inc(q_by_j_ready, 1)
                if live(0):
                    n = i
                    act.wait_ge(kT_ps, n + 1)
                    wait(act, kv_ps, n)
                    nc.scalar.activation(k_tok[:, :, :], pKT, ACT.Copy).then_inc(k_tok_ready, 1)

            all_steps(act, step)

        @block.vector
        def _(dve):
            nc.vector.memset(v_bd[:, :, :, :, :], 0.0).then_inc(dve_setup, 1)
            nc.vector.memset(x1T[:, 0:1], 0.0)
            dve.wait_ge(dve_setup, 1)
            for b in range(NB):
                for r in range(2):
                    last = nc.vector.memset(v_bd[C * b:C * b + C, r, :, b, :].rearrange(
                        "p t (h e) -> p t h e", e=V1)[:, :, :, D:V1], 1.0)
            last.then_inc(v_bd_zeroed, 1)
            nc.vector.memset(q_bd[:, H // 2:H, :], 0.0).then_inc(q_bd_zeroed, 1)
            nc.vector.memset(state_bd[:, :, :, :], 0.0).then_inc(state_bd_zeroed, 1)
            dve.wait_ge(w_loaded, 7 * DMA)
            nc.vector.tensor_copy(wp_in[:, :].rearrange("p (j g e) -> p j g e", j=J, g=G),
                                  w_in[:, WP, :].rearrange("p (g j e) -> p j g e", g=G, j=J)).then_inc(wp_permuted, 1)
            nc.vector.tensor_scalar(one_minus_mu[:, :], mu[:, :], -1.0, 1.0, ALU.mult, ALU.add).then_inc(dve_setup, 1)
            dve.wait_ge(dve_setup, 2)
            dve.wait_ge(pool_setup, CONSTS)

            def normalize_attention(n):
                dve.wait_ge(av_ps, n + 1)
                flat = pAV.rearrange("p k t b (g e) -> p k (t b g) e", e=V1)
                halves = lambda a: a[:, :].rearrange("p (k c) -> p k c", k=2)
                nc.vector.tensor_scalar(halves(den), flat[:, :, :, D], DEN_EPS, None, ALU.add).then_inc(den_ready, 1)
                dve.wait_ge(den_ready, n + 1)
                nc.vector.reciprocal(rden[:, :], den[:, :]).then_inc(rden_ready, 1)
                dve.wait_ge(rden_ready, n + 1)
                nc.vector.tensor_tensor(y[:, :].rearrange("p (k a e) -> p k a e", k=2, e=D), flat[:, :, :, 0:D],
                                        halves(rden).unsqueeze(3).broadcast_to([E, 2, C, D]),
                                        ALU.mult).then_inc(y_ready, 1)
                dve.wait_ge(y_ready, n + 1)
                wait(dve, wp_ps, n)
                nc.vector.transpose(yT[:, :], y[:, :]).then_inc(yT_ready, 1)

            def mask_scores(n, t):
                dve.wait_ge(A_ps, TT * n + t + 1)
                if t == 0:
                    wait(dve, av_ps, n)
                nc.vector.tensor_tensor(A_sb[:, t, :, :], pA[:, t % 2, :, :],
                                        causal[:, :].unsqueeze(1).broadcast_to([E, H, C]),
                                        ALU.mult).then_inc(A_masked, 1)

            def step(i, par, live):
                if live(4):
                    n = i - 4
                    dve.wait_ge(z2_ready, n + 1)
                    for t in range(TT):
                        nc.vector.bn_stats(stats[:, TT + t, :], z2[:, t, :]).then_inc(stats2_ready, 1)
                if live(3) or live(4):
                    m, cols = i - 3, norm_columns(live)
                    twice_mean, diff, cv, diff2, within = (moments[:, k, cols] for k in range(5))
                    if live(4):
                        dve.wait_ge(stats2_ready, TT * m)
                    else:
                        dve.wait_ge(stats1_ready, TT * (m + 1))
                    nc.vector.tensor_tensor(diff, stats[:, cols, 1], stats[:, cols, 4],
                                            ALU.subtract).then_inc(moments_ready, 1)
                    nc.vector.tensor_tensor(cv, stats[:, cols, 2], stats[:, cols, 5],
                                            ALU.add).then_inc(moments_ready, 1)
                    nc.vector.tensor_tensor(twice_mean, stats[:, cols, 1], stats[:, cols, 4],
                                            ALU.add).then_inc(moments_ready, 1)
                    dve.wait_ge(moments_ready, 5 * m + 3)
                    nc.vector.scalar_tensor_tensor(diff2, diff, 0.25, diff, ALU.mult, ALU.mult).then_inc(moments_ready, 1)
                    nc.vector.tensor_scalar(within, cv, 1.0 / E, LN_EPS, ALU.mult, ALU.add).then_inc(moments_ready, 1)
                    dve.wait_ge(moments_ready, 5 * (m + 1))
                    nc.vector.tensor_tensor(var[:, cols], diff2, within, ALU.add).then_inc(var_ready, 1)
                if live(1):
                    n = i - 1
                    dve.wait_ge(kv_ps, n + 1)
                    wait(dve, state_own_ready, n)
                    for k in range(2):
                        nc.vector.tensor_tensor_scan(state[:, 1 + KVH * k:1 + KVH * (k + 1)],
                                                     restart[:, :, :].rearrange("p n c -> p (n c)"),
                                                     pZ[:, k, 0:KVH], 0.0, ALU.mult, ALU.add).then_inc(state_ready, 1)
                if live(3) or live(4):
                    m, cols = i - 3, norm_columns(live)
                    dve.wait_ge(rstd_ready, m + 1)
                    nc.vector.scalar_tensor_tensor(shift[:, cols], moments[:, 0, cols], -0.5, rstd[:, cols],
                                                   ALU.mult, ALU.mult).then_inc(shift_ready, 1)
                if live(3):
                    n, p = i - 3, (par - 3) % 2
                    dve.wait_ge(shift_ready, n + 1)
                    wait(dve, z2_ready, n - 1)
                    for t in range(TT):
                        last = nc.vector.tensor_scalar(x1[:, p, t, :], z1[:, t, :], rstd[:, t:t + 1],
                                                       shift[:, t:t + 1], ALU.mult, ALU.add)
                    last.then_inc(x1_ready, 1)
                if live(2):
                    normalize_attention(i - 2)
                if live(3):
                    n = i - 3
                    dve.wait_ge(x1T_ready, n + 1)
                    wait(dve, k_ps, n)
                    for m in range(2):
                        nc.vector.scalar_tensor_tensor(mixed[:, m, :], x1T[:, 0:T], one_minus_mu[:, m:m + 1],
                                                       mu_x[:, m, :], ALU.mult, ALU.add).then_inc(mixed_ready, 1)
                if live(1):
                    mask_scores(i - 1, 0)
                if live(0):
                    n = i
                    dve.wait_ge(z_read, n + 1)
                    wait(dve, av_ps, n - 1)
                    nc.vector.scalar_tensor_tensor(phiT[:, par, :, :], e_z[:, :, :], 1.0, r_z[:, :, :],
                                                   ALU.min, ALU.add).then_inc(phi_ready, 1)
                if live(1):
                    mask_scores(i - 1, 1)
                    mask_scores(i - 1, 2)
                    mask_scores(i - 1, 3)
                if live(2):
                    n, p = i - 2, par
                    dve.wait_ge(wp_ps, n + 1)
                    dve.wait_ge(xb_ready, n + 1)
                    nc.vector.tensor_tensor(z1[:, :, :], pWP, xb[:, p, :, :], ALU.add).then_inc(z1_ready, 1)
                if live(3):
                    n = i - 3
                    dve.wait_ge(th_ready, n + 1)
                    dve.wait_ge(f_ps, n + 1)
                    wait(dve, z2_ready, n)
                    nc.vector.scalar_tensor_tensor(rk[:, :, :], th[:, :, :], 1.0, pF, ALU.add,
                                                   ALU.mult).then_inc(rk_ready, 1)
                if live(2):
                    n = i - 2
                    dve.wait_ge(z1_ready, n + 1)
                    for t in range(TT):
                        nc.vector.bn_stats(stats[:, t, :], z1[:, t, :]).then_inc(stats1_ready, 1)

            all_steps(dve, step)

        @block.tensor
        def _(pe):
            mm = nc.tensor.matmul
            pe.wait_ge(pool_setup, 2)
            for half, ws in enumerate(((WQ, WK, WV), (WP, WR, WFK, WFV))):
                if half == 0:
                    pe.wait_ge(qkv_loaded, 3 * DMA)
                else:
                    pe.wait_ge(w_loaded, 7 * DMA)
                    pe.wait_ge(wp_permuted, 1)
                dst = pA[:, half, :, :].rearrange("p h c -> p (h c)")
                for k, w in enumerate(ws):
                    src = wp_in[:, :] if w == WP else w_in[:, w, :]
                    last = nc.tensor.transpose(dst[:, E * k:E * (k + 1)], src, ident[:, :])
                last.then_inc(w_ps, 1)
            pe.wait_ge(w_ready, 3)

            def scores(n, p, t):
                if t == 0:
                    pe.wait_ge(q_bd_in, G * DMA * (n + 1))
                wait(pe, A_masked, TT * n + t - 1)
                for b in range(NB):
                    tok = E * t + C * b
                    last = mm(pA[C * b:C * b + C, t % 2, :, :], phiT[:, p, 1, tok:tok + C],
                              q_bd[:, :, tok:tok + C], start=True, stop=True)
                last.then_inc(A_ps, 1)

            def attend(n, p):
                for t in range(TT):
                    for g in range(G):
                        for j in range(J):
                            h = J * g + j
                            mm(pAV[C * j:C * j + C, t // 2, t % 2, :, V1 * g:V1 * g + V1], A_sb[:, t, h, :],
                               v_bd[:, p, t, :, V1 * h:V1 * h + V1], start=(t % 2 == 0 and g == 0), stop=False,
                               skip_group_check=True)
                pe.wait_ge(state_bd_in, G * DMA * (n + 1))
                for ch in range(1, NCH):
                    t, b = ch // NB, ch % NB
                    for j in range(J):
                        last = mm(pAV[C * j:C * j + C, t // 2, t % 2, b, :], phiT[:, p, 0, C * ch:C * ch + C],
                                  state_bd[:, :, ch - 1, V1 * j:V1 * j + V1], start=False,
                                  stop=(t % 2 == 1 and b == NB - 1), skip_group_check=True)
                last.then_inc(av_ps, 1)

            def step(i, par, live):
                if live(0):
                    n = i
                    pe.wait_ge(x_in, DMA * (n + 1))
                    wait(pe, k_tok_ready, n)
                    for t in range(TT):
                        last = nc.tensor.transpose(pXT[:, E * t:E * t + E], x_sb[:, par, t, :], ident[:, :])
                    last.then_inc(xT_ps, 1)
                if live(1):
                    n, p = i - 1, (par - 1) % 2
                    pe.wait_ge(v_ready, n + 1)
                    pe.wait_ge(k_tok_ready, n + 1)
                    for t in range(TT):
                        for g in range(G):
                            for k in range(2):
                                c0 = GV * g + GV // 2 * k
                                last = mm(pKV[C * g:C * g + C, k, t, :, :], k_tok[:, t, C * g:C * g + C],
                                          v_bd[:, p, t, :, c0:c0 + GV // 2], start=True, stop=True)
                    last.then_inc(kv_ps, 1)
                if live(2):
                    n = i - 2
                    pe.wait_ge(A_masked, TT * (n + 1))
                    wait(pe, z1_ready, n)
                    if live(1):
                        pe.wait_ge(v_ready, i)
                    attend(n, par)
                if live(3):
                    n, p = i - 3, (par - 3) % 2
                    pe.wait_ge(x1_ready, n + 1)
                    if live(0):
                        pe.wait_ge(xT_ready, i + 1)
                    else:
                        pe.wait_ge(k_tok_ready, B)
                        wait(pe, x1T_ready, n)
                    for t in range(TT):
                        last = nc.tensor.transpose(pX1T[:, E * t:E * t + E], x1[:, p, t, :], ident[:, :])
                    last.then_inc(x1T_ps, 1)
                if live(0):
                    n = i
                    pe.wait_ge(xT_ready, n + 1)
                    wait(pe, state_ready, 2 * n)
                    mm(pZ[:, 0, :], wT[:, WQ, :], xT[:, :], start=True, stop=True)
                    mm(pZ[:, 1, :], wT[:, WK, :], xT[:, :], start=True, stop=True).then_inc(z_ps, 1)
                if live(1):
                    scores(i - 1, (par - 1) % 2, 0)
                    scores(i - 1, (par - 1) % 2, 1)
                if live(0):
                    n = i
                    wait(pe, y_ready, n - 1)
                    for t in range(TT):
                        last = mm(pV[:, t, :], xT[:, E * t:E * t + E], wT[:, WV, :], start=True, stop=True)
                    last.then_inc(v_ps, 1)
                if live(3):
                    n = i - 3
                    if live(0):
                        pe.wait_ge(z_read, i + 1)
                    elif live(1):
                        pe.wait_ge(state_ready, 2 * i)
                    else:
                        pe.wait_ge(th_ready, n)
                    pe.wait_ge(mixed_ready, 2 * n + 1)
                    for t in range(TT):
                        last = mm(pR[:, t, :], mixed[:, 0, E * t:E * t + E], wT[:, WR, :], start=True, stop=True)
                    last.then_inc(r_ps, 1)
                    pe.wait_ge(mixed_ready, 2 * n + 2)
                    mm(pK, wT[:, WFK, :], mixed[:, 1, :], start=True, stop=True).then_inc(k_ps, 1)
                if live(1):
                    scores(i - 1, (par - 1) % 2, 2)
                    scores(i - 1, (par - 1) % 2, 3)
                if live(0):
                    n = i
                    pe.wait_ge(phi_ready, n + 1)
                    if live(3):
                        pe.wait_ge(x1T_ready, n - 2)
                    for t in range(TT):
                        last = nc.tensor.transpose(pKT[:, t, :], phiT[:, par, 1, E * t:E * t + E], ident[:, :])
                    last.then_inc(kT_ps, 1)
                if live(2):
                    n = i - 2
                    pe.wait_ge(yT_ready, n + 1)
                    for t in range(TT):
                        last = mm(pWP[:, t, :], yT[:, E * t:E * t + E], wT[:, WP, :], start=True, stop=True)
                    last.then_inc(wp_ps, 1)
                if live(3):
                    n = i - 3
                    pe.wait_ge(k_act_ready, n + 1)
                    wait(pe, rk_ready, n)
                    for t in range(TT):
                        last = mm(pF[:, t, :], k_act[:, E * t:E * t + E], wT[:, WFV, :], start=True, stop=True)
                    last.then_inc(f_ps, 1)

            all_steps(pe, step)


_INS = ["L0_attn_x", "L0_attn_Wq", "L0_attn_Wk", "L0_attn_Wv", "L0_attn_Wp", "L0_attn_bp",
        "L0_ffn_W_r", "L0_ffn_W_k", "L0_ffn_W_v", "L0_ffn_mu_r", "L0_ffn_mu_k"]


def kernel(**inputs):
    import numpy as _np
    import concourse.bacc as _bacc
    from concourse import mybir as _mybir
    from concourse.bass_utils import run_bass_kernel_spmd as _run

    nc = _bacc.Bacc("TRN2", target_bir_lowering=False, num_devices=1)
    arrays, args = {}, []
    for name in _INS:
        a = _np.ascontiguousarray(inputs[name])
        arrays[f"in_{name}"] = a
        args.append(nc.dram_tensor(f"in_{name}", a.shape, _mybir.dt.from_np(a.dtype), kind="ExternalInput").ap())
    shape = arrays["in_L0_attn_x"].shape
    args.append(nc.dram_tensor("out_0", shape, _mybir.dt.float32, kind="ExternalOutput").ap())
    postln_block_kernel(nc, *args)
    r = _run(nc, [arrays], core_ids=[0])
    return r.results[0]["out_0"]
```

```python
import concourse.bass as bass
from concourse import mybir
from contextlib import ExitStack

F32 = mybir.dt.float32
F32R = mybir.dt.float32r
ALU = mybir.AluOpType
ACT = mybir.ActivationFunctionType


def postln_block_kernel(nc, x, Wq, Wk, Wv, Wp, bp, W_r, W_k, W_v, mu_r, mu_k, out):
    B, T, E = x.shape
    H, D = 16, 8
    C = 32
    G = J = 4
    TT = T // E
    NB = E // C
    NCH = T // C
    V1 = D + 1
    GV = J * V1
    HV = H * V1
    LAST = 4
    DEN_EPS, LN_EPS = 1e-6, 1e-5
    DMA = 16
    assert E == 128 and H * D == E and T == TT * E and G * J == H

    with ExitStack() as ctx:
        def sb(name, shape, dtype=F32):
            return ctx.enter_context(nc.sbuf_tensor(name, shape, dtype))

        def ps(name, shape):
            return ctx.enter_context(nc.psum_tensor(name, shape, F32))

        def sem(name):
            return ctx.enter_context(nc.semaphore(name))

        ident = sb("ident", [E, E])
        causal = sb("causal", [E, C])
        head_of_group = sb("head_of_group", [E, J])
        state_mask = sb("state_mask", [E, GV])
        restart = sb("restart", [E, GV, NCH // 2])
        minus_half = sb("minus_half", [E, 2 * TT])
        bias_row = sb("bias_row", [E, E])
        mu = sb("mu", [E, 2])
        one_minus_mu = sb("one_minus_mu", [E, 2])
        w_in = sb("w_in", [E, 7, E])
        wp_in = sb("wp_in", [E, E])
        wT = sb("wT", [E, 7, E])
        w_high = sb("w_high", [E, 2, E], F32R)
        w_low = sb("w_low", [E, 2, E], F32R)
        WQ, WK, WV, WP, WR, WFK, WFV = range(7)
        MU_R, MU_K = range(2)

        x_sb = sb("x_sb", [E, 2, TT, E])
        xT = sb("xT", [E, T])
        xT_high = sb("xT_high", [E, T], F32R)
        xT_low = sb("xT_low", [E, T], F32R)
        e_z = sb("e_z", [E, 2, T])
        r_z = sb("r_z", [E, 2, T])
        phiT = sb("phiT", [E, 2, 2, T])
        q_by_j = sb("q_by_j", [E, J, T])
        q_bd = sb("q_bd", [E, H, T])
        k_tok = sb("k_tok", [E, TT, E])
        v_bd = sb("v_bd", [E, 2, TT, NB, HV])
        A_sb = sb("A_sb", [E, TT, H, C])
        state = sb("state", [E, 2, GV, NCH // 2])
        state_own = sb("state_own", [E, NCH, GV])
        state_bd = sb("state_bd", [E, G, NCH - 1, GV])
        den = sb("den", [E, 2 * C])
        rden = sb("rden", [E, 2 * C])
        y = sb("y", [E, T])
        yT = sb("yT", [E, T])
        xb = sb("xb", [E, 2, TT, E])
        z1 = sb("z1", [E, TT, E])
        x1 = sb("x1", [E, 2, TT, E])
        x1T = sb("x1T", [E, T + 1])
        mu_x = sb("mu_x", [E, 2, T])
        mixed = sb("mixed", [E, 2, T])
        th = sb("th", [E, TT, E])
        k_relu = sb("k_relu", [E, T])
        k_act = sb("k_act", [E, T])
        rk = sb("rk", [E, TT, E])
        z2 = sb("z2", [E, 2, TT, E])
        stats = sb("stats", [E, 2 * TT, 6])
        moments = sb("moments", [E, 5, 2 * TT])
        var = sb("var", [E, 2 * TT])
        rstd = sb("rstd", [E, 2 * TT])
        shift = sb("shift", [E, 2 * TT])
        o_sb = sb("o_sb", [E, 2, TT, E])

        pA = ps("pA", [E, 2, H, C])
        pZ = ps("pZ", [E, 2, T])
        pW = ps("pW", [E, 4, T])

        def tiles(bank):
            return pW[:, bank, :].rearrange("p (t f) -> p t f", t=TT)

        pXT, pX1T, pKT, pV, pWP, pF = pW[:, 2, :], pW[:, 0, :], tiles(0), tiles(1), tiles(2), tiles(3)
        pK, pR = pW[:, 3, :], tiles(0)
        pK_last, pR_last = pZ[:, 1, :], pZ[:, 0, :].rearrange("p (t f) -> p t f", t=TT)
        pAV = pW[:, 1:3, 0:2 * HV].rearrange("p k (t b n) -> p k t b n", t=2, b=NB)

        def w_ps_view(half):
            return pA[:, half, :, :].rearrange("p h c -> p (h c)").rearrange("p (k f) -> p k f", k=4)

        KVH = GV * NCH // 2
        pKV = pZ[:, :, 0:KVH].rearrange("p k (n t b) -> p k t b n", t=TT // 2, b=NB)

        IDENT_DONE = 2
        HEADS_DONE = 3 + 2 * (E // C)
        CONSTS = 8 + 5 * (E // C)
        J_DVE = 3
        Q_POOL, Q_ACT = H // 4, 3 * H // 4
        qkv_loaded, w_loaded, wp_permuted, pool_setup = sem("qkv_loaded"), sem("w_loaded"), sem("wp_permuted"), sem("pool_setup")
        w_ps, w_ready, dve_setup = sem("w_ps"), sem("w_ready"), sem("dve_setup")
        v_bd_zeroed, q_bd_zeroed, state_bd_zeroed = sem("v_bd_zeroed"), sem("q_bd_zeroed"), sem("state_bd_zeroed")
        x_in, out_done, q_bd_in, state_bd_in = sem("x_in"), sem("out_done"), sem("q_bd_in"), sem("state_bd_in")
        w_low_ready, xT_low_ready = sem("w_low_ready"), sem("xT_low_ready")
        xT_ps, z_ps, v_ps, kT_ps, A_ps = sem("xT_ps"), sem("z_ps"), sem("v_ps"), sem("kT_ps"), sem("A_ps")
        av_ps, kv_ps, wp_ps, x1T_ps = sem("av_ps"), sem("kv_ps"), sem("wp_ps"), sem("x1T_ps")
        r_ps, k_ps, f_ps = sem("r_ps"), sem("k_ps"), sem("f_ps")
        xT_ready, z_read, v_ready, q_by_j_act = sem("xT_ready"), sem("z_read"), sem("v_ready"), sem("q_by_j_act")
        k_tok_ready, x1T_ready, th_ready = sem("k_tok_ready"), sem("x1T_ready"), sem("th_ready")
        relu_ready, o_ready = sem("relu_ready"), sem("o_ready")
        phi_ready, A_masked, den_ready = sem("phi_ready"), sem("A_masked"), sem("den_ready")
        q_by_j_dve = sem("q_by_j_dve")
        rden_ready, y_ready, yT_ready, state_ready = sem("rden_ready"), sem("y_ready"), sem("yT_ready"), sem("state_ready")
        mixed_ready, z1_ready = sem("mixed_ready"), sem("z1_ready")
        stats1_ready, stats2_ready = sem("stats1_ready"), sem("stats2_ready")
        moments_ready, var_ready, shift_ready = sem("moments_ready"), sem("var_ready"), sem("shift_ready")
        x1_ready, rk_ready = sem("x1_ready"), sem("rk_ready")
        xb_ready, state_own_ready, k_act_ready = sem("xb_ready"), sem("state_own_ready"), sem("k_act_ready")
        z2_ready, rstd_ready = sem("z2_ready"), sem("rstd_ready")
        last_tiles_ready = sem("last_tiles_ready")

        def wait(eng, s, value):
            if not isinstance(value, int) or value > 0:
                eng.wait_ge(s, value)

        def held(eng, value):
            if not isinstance(value, int):
                eng.compute_val(value)
            return value

        FIRST_LOOPED = LAST + 1
        LOOP_END = B - 1
        DRAINED = B + 1
        assert (LOOP_END - FIRST_LOOPED) % 2 == 0

        def all_steps(eng, step, last_steps):
            for i in range(FIRST_LOOPED):
                step(i, i % 2, lambda lag, i=i: 0 <= i - lag < B)
            with eng.Fori(0, (LOOP_END - FIRST_LOOPED) // 2) as pair:
                for k in range(2):
                    step(pair * 2 + (FIRST_LOOPED + k), (FIRST_LOOPED + k) % 2, lambda lag: True)
            for i in range(LOOP_END, DRAINED):
                step(i, i % 2, lambda lag, i=i: 0 <= i - lag < B)
            last_steps()

        FIRST, SECOND, BOTH = slice(0, TT), slice(TT, 2 * TT), slice(0, 2 * TT)
        LAST_ROUNDS = {(B - 2, 1): B - 2, (B - 1, 1): B - 1, (B - 3, 2): B, (B - 2, 2): B + 1, (B - 1, 2): B + 2}

        def round_of(n, norm):
            usual = n if norm == 1 else n + 1
            return LAST_ROUNDS.get((n, norm), usual) if isinstance(n, int) else usual

        block = ctx.enter_context(nc.Block())

        @block.sync
        def _(sp):
            weights = tuple(enumerate((Wq, Wk, Wv, Wp, W_r, W_k, W_v)))
            sp.dma_start(x_sb[:, 0, :, :], x[0, :, :].rearrange("(t p) f -> p t f", p=E)).then_inc(x_in, DMA)
            for k, w in weights[:3]:
                sp.dma_start(w_in[:, k, :], w[:, :]).then_inc(qkv_loaded, DMA)
            for k, w in weights[3:]:
                sp.dma_start(w_in[:, k, :], w[:, :]).then_inc(w_loaded, DMA)
            sp.dma_start(bias_row[:, :], bp.rearrange("(a f) -> a f", a=1).broadcast_to([E, E])).then_inc(w_loaded, DMA)
            sp.dma_start(mu[:, 0:1], mu_r.rearrange("(f a) -> f a", a=1)).then_inc(w_loaded, DMA)
            sp.dma_start(mu[:, 1:2], mu_k.rearrange("(f a) -> f a", a=1)).then_inc(w_loaded, DMA)

            def store(n, par):
                row, done, stored = held(sp, n), held(sp, n + 1), held(sp, DMA * n)
                held(sp, n * (T * E) * 4)
                wait(sp, out_done, stored)
                sp.wait_ge(o_ready, done)
                sp.dma_start(out[row, :, :].rearrange("(t p) f -> p t f", p=E),
                             o_sb[:, par, :, :]).then_inc(out_done, DMA)

            def step(i, par, live):
                if live(1):
                    n, own = held(sp, i - 1), held(sp, i)
                    if not live(2):
                        sp.wait_ge(state_bd_zeroed, 1)
                    wait(sp, av_ps, n)
                    sp.wait_ge(state_own_ready, own)
                    for g in range(G):
                        sp.dma_start(state_bd[C * g:C * g + C, g, :, :],
                                     state_own[C * g:C * g + C, 0:NCH - 1, :]).then_inc(state_bd_in, DMA)
                if live(4):
                    store(i - 4, par)
                if live(-1):
                    n, used = held(sp, i + 1), held(sp, i)
                    held(sp, (i + 1) * (T * E) * 4)
                    wait(sp, xb_ready, used)
                    wait(sp, xT_ps, n)
                    sp.dma_start(x_sb[:, (par + 1) % 2, :, :],
                                 x[n, :, :].rearrange("(t p) f -> p t f", p=E)).then_inc(x_in, DMA)
                if live(0):
                    used, ready = held(sp, TT * i), held(sp, i + 1)
                    if not live(1):
                        sp.wait_ge(q_bd_zeroed, 3)
                    wait(sp, A_ps, used)
                    sp.wait_ge(q_by_j_act, ready)
                    sp.wait_ge(q_by_j_dve, ready)
                    for g in range(G):
                        sp.dma_start(q_bd[C * g:C * g + C, J * g:J * g + J, :],
                                     q_by_j[C * g:C * g + C, :, :]).then_inc(q_bd_in, DMA)

            def last_steps():
                for n in range(B - 3, B):
                    if n == B - 1:
                        sp.wait_ge(last_tiles_ready, 1)
                    store(n, n % 2)

            all_steps(sp, step, last_steps)
            sp.wait_ge(out_done, DMA * B)

        @block.gpsimd
        def _(pool):
            done = [0]

            def alone(ins):
                done[0] += 1
                ins.then_inc(pool_setup, 1)
                pool.wait_ge(pool_setup, done[0])

            def select(t, rows, compare, fill, base, pattern, step):
                alone(nc.gpsimd.affine_select(out=t[rows, :], in_=t[rows, :], compare_op=compare, fill=fill,
                                              base=base, pattern=pattern, channel_multiplier=step))

            quadrants = [slice(C * q, C * q + C) for q in range(E // C)]
            alone(nc.gpsimd.memset(ident[:, :], 0.0))
            select(ident, slice(0, E), ALU.not_equal, 1.0, 0, [[-1, E]], 1)
            alone(nc.gpsimd.memset(head_of_group[:, :], 1.0))
            for rows in quadrants:
                select(head_of_group, rows, ALU.is_ge, 0.0, 0, [[-D, J]], 1)
                select(head_of_group, rows, ALU.is_ge, 0.0, D - 1, [[D, J]], -1)
            assert done[0] == HEADS_DONE
            nc.gpsimd.memset(q_bd[:, 0:Q_POOL, :], 0.0).then_inc(q_bd_zeroed, 1)
            alone(nc.gpsimd.memset(state_mask[:, :], 1.0))
            for rows in quadrants:
                select(state_mask, rows, ALU.is_ge, 0.0, 0, [[-D, J], [0, V1]], 1)
                select(state_mask, rows, ALU.is_ge, 0.0, D - 1, [[D, J], [0, V1]], -1)
            alone(nc.gpsimd.memset(causal[:, :], 1.0))
            for rows in quadrants:
                select(causal, rows, ALU.is_ge, 0.0, 0, [[1, C]], -1)
            alone(nc.gpsimd.memset(minus_half[:, :], -0.5))
            alone(nc.gpsimd.memset(restart[:, :, :], 1.0))
            alone(nc.gpsimd.memset(restart[:, :, 0:1], 0.0))
            assert done[0] == CONSTS

            def second_residual(n, p):
                pool.wait_ge(rk_ready, n + 1)
                wait(pool, o_ready, n - 1)
                nc.gpsimd.tensor_tensor(z2[:, p, :, :], rk[:, :, :], x1[:, p, :, :], ALU.add).then_inc(z2_ready, 1)

            def square(n):
                pool.wait_ge(relu_ready, n + 1)
                wait(pool, f_ps, n)
                nc.gpsimd.tensor_tensor(k_act[:, :], k_relu[:, :], k_relu[:, :], ALU.mult).then_inc(k_act_ready, 1)

            def inverse_deviation(m, cols, first_used, second_used):
                pool.wait_ge(var_ready, m + 1)
                wait(pool, x1_ready, first_used)
                wait(pool, o_ready, second_used)
                nc.gpsimd.tensor_tensor(rstd[:, cols], var[:, cols], minus_half[:, cols],
                                        ALU.pow).then_inc(rstd_ready, 1)

            def step(i, par, live):
                if live(4):
                    second_residual(i - 4, par)
                if live(3):
                    inverse_deviation(i - 3, BOTH if live(4) else FIRST, i - 3, i - 4)
                if live(1):
                    n = i - 1
                    if not live(2):
                        pool.wait_ge(w_loaded, 7 * DMA)
                    pool.wait_ge(state_ready, 3 * (n + 1))
                    wait(pool, state_bd_in, G * DMA * n)
                    nc.gpsimd.tensor_tensor(state_own[:, :, :].rearrange("p (k c) n -> p k c n", k=2),
                                            state[:, :, :, :].rearrange("p k n c -> p k c n"),
                                            state_mask[:, :].unsqueeze(1).unsqueeze(1).broadcast_to([E, 2, NCH // 2, GV]),
                                            ALU.mult).then_inc(state_own_ready, 1)
                if live(1):
                    n, p = i - 1, (par - 1) % 2
                    pool.wait_ge(xT_ps, n + 1)
                    wait(pool, z1_ready, n - 1)
                    nc.gpsimd.tensor_tensor(xb[:, p, :, :], x_sb[:, p, :, :],
                                            bias_row[:, :].unsqueeze(1).broadcast_to([E, TT, E]),
                                            ALU.add).then_inc(xb_ready, 1)
                if live(3):
                    square(i - 3)

            def last_steps():
                inverse_deviation(round_of(B - 2, 1), FIRST, B - 2, 0)
                second_residual(B - 3, (B - 3) % 2)
                square(B - 2)
                inverse_deviation(round_of(B - 1, 1), FIRST, B - 1, 0)
                inverse_deviation(round_of(B - 3, 2), SECOND, 0, B - 3)
                inverse_deviation(round_of(B - 2, 2), SECOND, 0, B - 2)
                inverse_deviation(round_of(B - 1, 2), SECOND, 0, B - 1)

            all_steps(pool, step, last_steps)

        @block.scalar
        def _(act):
            def second_norm(n, par, tiles_of_row=range(TT)):
                act.wait_ge(shift_ready, round_of(n, 2) + 1)
                wait(act, out_done, DMA * (n - 1))
                for t in tiles_of_row:
                    last = nc.scalar.activation(o_sb[:, par, t, :], z2[:, par, t, :], ACT.Identity,
                                                bias=shift[:, TT + t:TT + t + 1], scale=rstd[:, TT + t:TT + t + 1])
                last.then_inc(o_ready, 1)

            def mix_input_k(n):
                act.wait_ge(x1T_ps, n + 1)
                wait(act, mixed_ready, 2 * n)
                nc.scalar.activation(x1T[:, 1:T + 1], pX1T, ACT.Copy)
                nc.scalar.activation(mu_x[:, MU_K, :], pX1T, ACT.Copy, scale=mu[:, MU_K:MU_K + 1]).then_inc(x1T_ready, 1)

            def mix_input_r():
                nc.scalar.activation(mu_x[:, MU_R, :], pX1T, ACT.Copy, scale=mu[:, MU_R:MU_R + 1]).then_inc(x1T_ready, 1)

            def relu_k(n, k):
                act.wait_ge(k_ps, n + 1)
                wait(act, k_act_ready, n)
                nc.scalar.activation(k_relu[:, :], k, ACT.Relu).then_inc(relu_ready, 1)

            def tanh_r(n, r):
                act.wait_ge(r_ps, n + 1)
                wait(act, rk_ready, n)
                nc.scalar.activation(th[:, :, :], r, ACT.Tanh, scale=0.5).then_inc(th_ready, 1)

            def step(i, par, live):
                if live(0):
                    n = i
                    act.wait_ge(xT_ps, n + 1)
                    wait(act, v_ps, n)
                    wait(act, xT_low_ready, n)
                    nc.scalar.activation(xT_high[:, :], pXT, ACT.Copy)
                    nc.scalar.activation(xT[:, :], pXT, ACT.Copy).then_inc(xT_ready, 1)
                if not live(1) and live(0):
                    act.wait_ge(w_ps, 1)
                    nc.scalar.activation(w_high[:, :, :], w_ps_view(0)[:, 0:2, :], ACT.Copy)
                    nc.scalar.activation(wT[:, 0:3, :], w_ps_view(0)[:, 0:3, :], ACT.Copy).then_inc(w_ready, 1)
                    nc.scalar.activation(q_bd[:, Q_POOL:Q_ACT, :],
                                         ident[:, 0:1].unsqueeze(2).broadcast_to([E, Q_ACT - Q_POOL, T]),
                                         ACT.Copy, scale=0.0).then_inc(q_bd_zeroed, 1)
                if live(4):
                    second_norm(i - 4, par)
                if live(3):
                    mix_input_k(i - 3)
                    mix_input_r()
                if live(0):
                    n = i
                    act.wait_ge(z_ps, n + 1)
                    wait(act, phi_ready, n)
                    nc.scalar.activation(e_z[:, :, :], pZ[:, :, :], ACT.Exp)
                    nc.scalar.activation(r_z[:, :, :], pZ[:, :, :], ACT.Relu).then_inc(z_read, 1)
                if live(3):
                    relu_k(i - 3, pK)
                    tanh_r(i - 3, pR)
                if live(0):
                    n = i
                    if not live(1):
                        act.wait_ge(v_bd_zeroed, 1)
                    act.wait_ge(v_ps, n + 1)
                    wait(act, av_ps, n - 1)
                    for b in range(NB):
                        rows = slice(C * b, C * b + C)
                        last = nc.scalar.activation(
                            v_bd[rows, par, :, b, :].rearrange("p t (h e) -> p t h e", e=V1)[:, :, :, 0:D],
                            pV[rows, :, :].rearrange("p t (h e) -> p t h e", e=D), ACT.Copy)
                    last.then_inc(v_ready, 1)
                if not live(1) and live(0):
                    act.wait_ge(w_ps, 2)
                    nc.scalar.activation(wT[:, 3:6, :], w_ps_view(1)[:, 0:3, :], ACT.Copy)
                    nc.scalar.activation(wT[:, 6, :], w_ps_view(1)[:, 3, :], ACT.Copy, scale=0.5).then_inc(w_ready, 1)
                    act.wait_ge(w_loaded, 7 * DMA)
                if live(0):
                    n = i
                    act.wait_ge(kT_ps, n + 1)
                    wait(act, kv_ps, n)
                    nc.scalar.activation(k_tok[:, :, :], pKT, ACT.Copy).then_inc(k_tok_ready, 1)
                if live(0):
                    n = i
                    if not live(1):
                        act.wait_ge(pool_setup, HEADS_DONE)
                    act.wait_ge(phi_ready, n + 1)
                    wait(act, q_bd_in, G * DMA * n)
                    for j in range(J_DVE, J):
                        last = nc.scalar.activation(q_by_j[:, j, :], phiT[:, par, 0, :], ACT.Copy,
                                                    scale=head_of_group[:, j:j + 1])
                    last.then_inc(q_by_j_act, 1)

            def last_steps():
                mix_input_k(B - 2)
                mix_input_r()
                relu_k(B - 2, pK_last)
                tanh_r(B - 2, pR_last)
                mix_input_k(B - 1)
                mix_input_r()
                second_norm(B - 3, (B - 3) % 2)
                relu_k(B - 1, pK_last)
                tanh_r(B - 1, pR_last)
                second_norm(B - 2, (B - 2) % 2)
                second_norm(B - 1, (B - 1) % 2, range(TT // 2))

            all_steps(act, step, last_steps)

        @block.vector
        def _(dve):
            nc.vector.memset(v_bd[:, :, :, :, :], 0.0).then_inc(dve_setup, 1)
            nc.vector.memset(x1T[:, 0:1], 0.0)

            def rest_of_setup():
                dve.wait_ge(dve_setup, 1)
                for b in range(NB):
                    for r in range(2):
                        last = nc.vector.memset(v_bd[C * b:C * b + C, r, :, b, :].rearrange(
                            "p t (h e) -> p t h e", e=V1)[:, :, :, D:V1], 1.0)
                last.then_inc(v_bd_zeroed, 1)
                nc.vector.memset(q_bd[:, Q_ACT:H, :], 0.0).then_inc(q_bd_zeroed, 1)
                dve.wait_ge(w_loaded, 7 * DMA)
                nc.vector.tensor_copy(wp_in[:, :].rearrange("p (j g e) -> p j g e", j=J, g=G),
                                      w_in[:, WP, :].rearrange("p (g j e) -> p j g e", g=G, j=J)).then_inc(wp_permuted, 1)
                nc.vector.tensor_scalar(one_minus_mu[:, :], mu[:, :], -1.0, 1.0, ALU.mult, ALU.add).then_inc(dve_setup, 1)

            def low_part(dst, full, high):
                return nc.vector.tensor_tensor(dst, full, high.bitcast(F32), ALU.subtract)

            def stats_of_first(n):
                dve.wait_ge(z1_ready, n + 1)
                for t in range(TT):
                    nc.vector.bn_stats(stats[:, t, :], z1[:, t, :]).then_inc(stats1_ready, 1)

            def stats_of_second(n, p):
                dve.wait_ge(z2_ready, n + 1)
                for t in range(TT):
                    nc.vector.bn_stats(stats[:, TT + t, :], z2[:, p, t, :]).then_inc(stats2_ready, 1)

            def variances(m, cols, stats_ready, stats_value):
                twice_mean, diff, cv, diff2, within = (moments[:, k, cols] for k in range(5))
                dve.wait_ge(stats_ready, stats_value)
                nc.vector.tensor_tensor(diff, stats[:, cols, 1], stats[:, cols, 4],
                                        ALU.subtract).then_inc(moments_ready, 1)
                nc.vector.tensor_tensor(cv, stats[:, cols, 2], stats[:, cols, 5],
                                        ALU.add).then_inc(moments_ready, 1)
                nc.vector.tensor_tensor(twice_mean, stats[:, cols, 1], stats[:, cols, 4],
                                        ALU.add).then_inc(moments_ready, 1)
                dve.wait_ge(moments_ready, 5 * m + 3)
                nc.vector.scalar_tensor_tensor(diff2, diff, 0.25, diff, ALU.mult, ALU.mult).then_inc(moments_ready, 1)
                nc.vector.tensor_scalar(within, cv, 1.0 / E, LN_EPS, ALU.mult, ALU.add).then_inc(moments_ready, 1)
                dve.wait_ge(moments_ready, 5 * (m + 1))
                nc.vector.tensor_tensor(var[:, cols], diff2, within, ALU.add).then_inc(var_ready, 1)

            def shifts(m, cols):
                dve.wait_ge(rstd_ready, m + 1)
                nc.vector.scalar_tensor_tensor(shift[:, cols], moments[:, 0, cols], -0.5, rstd[:, cols],
                                               ALU.mult, ALU.mult).then_inc(shift_ready, 1)

            def first_norm(n, p):
                dve.wait_ge(shift_ready, round_of(n, 1) + 1)
                wait(dve, z2_ready, n - 1)
                for t in range(TT):
                    last = nc.vector.tensor_scalar(x1[:, p, t, :], z1[:, t, :], rstd[:, t:t + 1],
                                                   shift[:, t:t + 1], ALU.mult, ALU.add)
                last.then_inc(x1_ready, 1)

            def normalize_attention(n):
                dve.wait_ge(av_ps, n + 1)
                flat = pAV.rearrange("p k t b (g e) -> p k (t b g) e", e=V1)
                halves = lambda a: a[:, :].rearrange("p (k c) -> p k c", k=2)
                nc.vector.tensor_scalar(halves(den), flat[:, :, :, D], DEN_EPS, None, ALU.add).then_inc(den_ready, 1)
                dve.wait_ge(den_ready, n + 1)
                nc.vector.reciprocal(rden[:, :], den[:, :]).then_inc(rden_ready, 1)
                dve.wait_ge(rden_ready, n + 1)
                nc.vector.tensor_tensor(y[:, :].rearrange("p (k a e) -> p k a e", k=2, e=D), flat[:, :, :, 0:D],
                                        halves(rden).unsqueeze(3).broadcast_to([E, 2, C, D]),
                                        ALU.mult).then_inc(y_ready, 1)
                dve.wait_ge(y_ready, n + 1)
                wait(dve, wp_ps, n)
                nc.vector.transpose(yT[:, :], y[:, :]).then_inc(yT_ready, 1)

            def mix(n, m):
                wait(dve, k_ps if m == MU_K else r_ps, n)
                dve.wait_ge(x1T_ready, 2 * n + (1 if m == MU_K else 2))
                nc.vector.scalar_tensor_tensor(mixed[:, m, :], x1T[:, 0:T], one_minus_mu[:, m:m + 1],
                                               mu_x[:, m, :], ALU.mult, ALU.add).then_inc(mixed_ready, 1)

            def mask_scores(n, t):
                dve.wait_ge(A_ps, TT * n + t + 1)
                if t == 0:
                    wait(dve, av_ps, n)
                nc.vector.tensor_tensor(A_sb[:, t, :, :], pA[:, t % 2, :, :],
                                        causal[:, :].unsqueeze(1).broadcast_to([E, H, C]),
                                        ALU.mult).then_inc(A_masked, 1)

            def first_residual(n, p):
                dve.wait_ge(wp_ps, n + 1)
                dve.wait_ge(xb_ready, n + 1)
                nc.vector.tensor_tensor(z1[:, :, :], pWP, xb[:, p, :, :], ALU.add).then_inc(z1_ready, 1)

            def gated(n):
                dve.wait_ge(th_ready, n + 1)
                dve.wait_ge(f_ps, n + 1)
                wait(dve, z2_ready, n)
                nc.vector.scalar_tensor_tensor(rk[:, :, :], th[:, :, :], 1.0, pF, ALU.add,
                                               ALU.mult).then_inc(rk_ready, 1)

            def step(i, par, live):
                def split_x():
                    n = i
                    dve.wait_ge(xT_ready, n + 1)
                    wait(dve, z_ps, n)
                    low_part(xT_low[:, :], xT[:, :], xT_high[:, :]).then_inc(xT_low_ready, 1)

                if live(0) and not live(3):
                    split_x()
                if not live(1) and live(0):
                    dve.wait_ge(w_ready, 1)
                    low_part(w_low[:, :, :], wT[:, 0:2, :], w_high[:, :, :]).then_inc(w_low_ready, 1)
                    rest_of_setup()
                if live(4):
                    stats_of_second(i - 4, par)
                    variances(i - 3, BOTH, stats2_ready, TT * (i - 3))
                elif live(3):
                    variances(i - 3, FIRST, stats1_ready, TT * (i - 2))
                if live(1):
                    n = i - 1
                    if not live(2):
                        dve.wait_ge(pool_setup, CONSTS)
                        dve.wait_ge(dve_setup, 2)
                    dve.wait_ge(kv_ps, n + 1)
                    wait(dve, state_own_ready, n)
                    for k in range(2):
                        if k == 1:
                            total = state[:, 0, :, NCH // 2 - 1]
                            chunk_8 = pKV[:, 1, 0, 0, :]
                            dve.wait_ge(state_ready, 3 * n + 1)
                            nc.vector.tensor_tensor(chunk_8, chunk_8, total, ALU.add).then_inc(state_ready, 1)
                            dve.wait_ge(state_ready, 3 * n + 2)
                        nc.vector.tensor_tensor_scan(state[:, k, :, :].rearrange("p n c -> p (n c)"),
                                                     restart[:, :, :].rearrange("p n c -> p (n c)"),
                                                     pZ[:, k, 0:KVH], 0.0, ALU.mult, ALU.add).then_inc(state_ready, 1)
                    if not live(2):
                        nc.vector.memset(state_bd[:, :, :, :], 0.0).then_inc(state_bd_zeroed, 1)
                if live(0) and live(3):
                    split_x()
                if live(3):
                    shifts(i - 3, BOTH if live(4) else FIRST)
                    first_norm(i - 3, (par - 3) % 2)
                if not live(0):
                    mask_scores(i - 1, 0)
                    mask_scores(i - 1, 1)
                if live(2):
                    normalize_attention(i - 2)
                if live(0) and live(1):
                    mask_scores(i - 1, 0)
                if live(3):
                    mix(i - 3, MU_K)
                    mix(i - 3, MU_R)
                if live(0) and live(1):
                    mask_scores(i - 1, 1)
                if not live(0):
                    mask_scores(i - 1, 2)
                    mask_scores(i - 1, 3)
                if live(2):
                    first_residual(i - 2, par)
                if live(0):
                    n = i
                    dve.wait_ge(z_read, n + 1)
                    wait(dve, av_ps, n - 1)
                    nc.vector.scalar_tensor_tensor(phiT[:, par, :, :], e_z[:, :, :], 1.0, r_z[:, :, :],
                                                   ALU.min, ALU.add).then_inc(phi_ready, 1)
                if live(0):
                    n = i
                    if not live(1):
                        dve.wait_ge(pool_setup, HEADS_DONE)
                    dve.wait_ge(phi_ready, n + 1)
                    wait(dve, q_bd_in, G * DMA * n)
                    for j in range(J_DVE):
                        last = nc.vector.tensor_scalar(q_by_j[:, j, :], phiT[:, par, 0, :], head_of_group[:, j:j + 1],
                                                       None, ALU.mult)
                    last.then_inc(q_by_j_dve, 1)
                if live(0) and live(1):
                    mask_scores(i - 1, 2)
                    mask_scores(i - 1, 3)
                if live(2) and not live(0):
                    stats_of_first(i - 2)
                if live(3) and live(0):
                    gated(i - 3)
                if live(2) and live(0):
                    stats_of_first(i - 2)

            def last_steps():
                def second_residual(n):
                    dve.wait_ge(rk_ready, n + 1)
                    dve.wait_ge(o_ready, n - 1)
                    nc.vector.tensor_tensor(z2[:, n % 2, :, :], rk[:, :, :], x1[:, n % 2, :, :], ALU.add).then_inc(z2_ready, 1)

                def variances_of_first(n):
                    variances(round_of(n, 1), FIRST, stats1_ready, TT * (n + 1))

                def variances_of_second(n):
                    variances(round_of(n, 2), SECOND, stats2_ready, TT * (n + 1))

                variances_of_first(B - 2)
                shifts(round_of(B - 2, 1), FIRST)
                first_norm(B - 2, (B - 2) % 2)
                normalize_attention(B - 1)
                gated(B - 3)
                mix(B - 2, MU_K)
                mix(B - 2, MU_R)
                first_residual(B - 1, (B - 1) % 2)
                stats_of_first(B - 1)
                variances_of_first(B - 1)
                stats_of_second(B - 3, (B - 3) % 2)
                variances_of_second(B - 3)
                shifts(round_of(B - 1, 1), FIRST)
                first_norm(B - 1, (B - 1) % 2)
                shifts(round_of(B - 3, 2), SECOND)
                gated(B - 2)
                second_residual(B - 2)
                mix(B - 1, MU_K)
                mix(B - 1, MU_R)
                stats_of_second(B - 2, (B - 2) % 2)
                dve.wait_ge(relu_ready, B)
                dve.wait_ge(f_ps, B - 1)
                nc.vector.tensor_tensor(k_act[:, :], k_relu[:, :], k_relu[:, :], ALU.mult).then_inc(k_act_ready, 1)
                variances_of_second(B - 2)
                shifts(round_of(B - 2, 2), SECOND)
                gated(B - 1)
                second_residual(B - 1)
                stats_of_second(B - 1, (B - 1) % 2)
                variances_of_second(B - 1)
                shifts(round_of(B - 1, 2), SECOND)
                dve.wait_ge(shift_ready, round_of(B - 1, 2) + 1)
                dve.wait_ge(out_done, DMA * (B - 2))
                for t in range(TT // 2, TT):
                    last = nc.vector.tensor_scalar(o_sb[:, (B - 1) % 2, t, :], z2[:, (B - 1) % 2, t, :],
                                                   rstd[:, TT + t:TT + t + 1], shift[:, TT + t:TT + t + 1],
                                                   ALU.mult, ALU.add)
                last.then_inc(last_tiles_ready, 1)

            all_steps(dve, step, last_steps)

        @block.tensor
        def _(pe):
            mm = nc.tensor.matmul

            def transpose_weights(half, ws):
                for k, w in enumerate(ws):
                    src = wp_in[:, :] if w == WP else w_in[:, w, :]
                    last = nc.tensor.transpose(w_ps_view(half)[:, k, :], src, ident[:, :])
                last.then_inc(w_ps, 1)

            def scores(n, p, t):
                if t == 0:
                    pe.wait_ge(q_bd_in, G * DMA * (n + 1))
                wait(pe, A_masked, TT * n + t - 1)
                for b in range(NB):
                    tok = E * t + C * b
                    last = mm(pA[C * b:C * b + C, t % 2, :, :], phiT[:, p, 1, tok:tok + C],
                              q_bd[:, :, tok:tok + C], start=True, stop=True)
                last.then_inc(A_ps, 1)

            def attend(n, p, xT_row=None):
                pe.wait_ge(A_masked, TT * (n + 1))
                wait(pe, z1_ready, n)
                for t in range(TT):
                    if t == TT // 2 and xT_row is not None:
                        pe.wait_ge(xT_ready, xT_row + 1)
                    for g in range(G):
                        for j in range(J):
                            h = J * g + j
                            mm(pAV[C * j:C * j + C, t // 2, t % 2, :, V1 * g:V1 * g + V1], A_sb[:, t, h, :],
                               v_bd[:, p, t, :, V1 * h:V1 * h + V1], start=(t % 2 == 0 and g == 0), stop=False,
                               skip_group_check=True)
                pe.wait_ge(state_bd_in, G * DMA * (n + 1))
                for ch in range(1, NCH):
                    t, b = ch // NB, ch % NB
                    for j in range(J):
                        last = mm(pAV[C * j:C * j + C, t // 2, t % 2, b, :], phiT[:, p, 0, C * ch:C * ch + C],
                                  state_bd[:, :, ch - 1, V1 * j:V1 * j + V1], start=False,
                                  stop=(t % 2 == 1 and b == NB - 1), skip_group_check=True)
                last.then_inc(av_ps, 1)

            def transpose_x1(n, p):
                pe.wait_ge(x1_ready, n + 1)
                for t in range(TT):
                    last = nc.tensor.transpose(pX1T[:, E * t:E * t + E], x1[:, p, t, :], ident[:, :])
                last.then_inc(x1T_ps, 1)

            def mix_product_k(n, dst):
                pe.wait_ge(mixed_ready, 2 * n + 1)
                mm(dst, wT[:, WFK, :], mixed[:, MU_K, :], start=True, stop=True).then_inc(k_ps, 1)

            def mix_product_r(n, dst):
                pe.wait_ge(mixed_ready, 2 * n + 2)
                for t in range(TT):
                    last = mm(dst[:, t, :], mixed[:, MU_R, E * t:E * t + E], wT[:, WR, :], start=True, stop=True)
                last.then_inc(r_ps, 1)

            def project_attention(n):
                pe.wait_ge(yT_ready, n + 1)
                for t in range(TT):
                    last = mm(pWP[:, t, :], yT[:, E * t:E * t + E], wT[:, WP, :], start=True, stop=True)
                last.then_inc(wp_ps, 1)

            def channel_mix_output(n):
                pe.wait_ge(k_act_ready, n + 1)
                for t in range(TT):
                    last = mm(pF[:, t, :], k_act[:, E * t:E * t + E], wT[:, WFV, :], start=True, stop=True)
                last.then_inc(f_ps, 1)

            def step(i, par, live):
                if live(0):
                    n = i
                    if not live(1):
                        pe.wait_ge(pool_setup, IDENT_DONE)
                    pe.wait_ge(x_in, DMA * (n + 1))
                    if live(3):
                        pe.wait_ge(z1_ready, n - 2)
                    for t in range(TT):
                        last = nc.tensor.transpose(pXT[:, E * t:E * t + E], x_sb[:, par, t, :], ident[:, :])
                    last.then_inc(xT_ps, 1)
                if not live(1) and live(0):
                    pe.wait_ge(qkv_loaded, 3 * DMA)
                    transpose_weights(0, (WQ, WK, WV))
                    pe.wait_ge(w_low_ready, 1)
                if live(1):
                    n, p = i - 1, (par - 1) % 2
                    pe.wait_ge(v_ready, n + 1)
                    pe.wait_ge(k_tok_ready, n + 1)
                    for t in range(TT):
                        for g in range(G):
                            last = mm(pKV[C * g:C * g + C, t // 2, t % 2, :, :], k_tok[:, t, C * g:C * g + C],
                                      v_bd[:, p, t, :, GV * g:GV * g + GV], start=True, stop=True)
                    last.then_inc(kv_ps, 1)
                if live(2):
                    if live(1):
                        pe.wait_ge(v_ready, i)
                    attend(i - 2, par, i if live(0) else None)
                def first_scores():
                    scores(i - 1, (par - 1) % 2, 0)
                    if not live(2):
                        pe.wait_ge(w_ready, 2)
                    scores(i - 1, (par - 1) % 2, 1)

                if live(2) and live(1):
                    first_scores()
                if live(3):
                    pe.wait_ge(k_tok_ready, i)
                    transpose_x1(i - 3, (par - 3) % 2)
                if live(0):
                    n = i
                    pe.wait_ge(xT_ready, n + 1)
                    wait(pe, state_ready, 3 * n)
                    pe.wait_ge(xT_low_ready, n + 1)
                    for w in (WQ, WK):
                        mm(pZ[:, w, :], w_high[:, w, :], xT_high[:, :], start=True, stop=False)
                        mm(pZ[:, w, :], w_low[:, w, :], xT_high[:, :], start=False, stop=False)
                        last = mm(pZ[:, w, :], w_high[:, w, :], xT_low[:, :], start=False, stop=True)
                    last.then_inc(z_ps, 1)
                if live(0):
                    n = i
                    wait(pe, y_ready, n - 1)
                    for t in range(TT):
                        last = mm(pV[:, t, :], xT[:, E * t:E * t + E], wT[:, WV, :], start=True, stop=True)
                    last.then_inc(v_ps, 1)
                if not live(2) and live(1):
                    first_scores()
                if not live(1) and live(0):
                    pe.wait_ge(w_loaded, 7 * DMA)
                    pe.wait_ge(wp_permuted, 1)
                    transpose_weights(1, (WP, WR, WFK, WFV))
                def last_scores():
                    scores(i - 1, (par - 1) % 2, 2)
                    scores(i - 1, (par - 1) % 2, 3)

                if not live(0):
                    last_scores()
                if live(2):
                    project_attention(i - 2)
                if live(3):
                    wait(pe, rk_ready, i - 3)
                    mix_product_k(i - 3, pK)
                    mix_product_r(i - 3, pR)
                if live(0) and live(1):
                    last_scores()
                if live(0):
                    n = i
                    pe.wait_ge(phi_ready, n + 1)
                    if live(3):
                        pe.wait_ge(th_ready, n - 2)
                    for t in range(TT):
                        last = nc.tensor.transpose(pKT[:, t, :], phiT[:, par, 1, E * t:E * t + E], ident[:, :])
                    last.then_inc(kT_ps, 1)
                if live(3) and live(0):
                    channel_mix_output(i - 3)

            def last_steps():
                attend(B - 1, (B - 1) % 2)
                pe.wait_ge(th_ready, B - 2)
                transpose_x1(B - 2, (B - 2) % 2)
                channel_mix_output(B - 3)
                project_attention(B - 1)
                pe.wait_ge(state_ready, 3 * B)
                mix_product_k(B - 2, pK_last)
                mix_product_r(B - 2, pR_last)
                pe.wait_ge(rk_ready, B - 2)
                channel_mix_output(B - 2)
                pe.wait_ge(x1T_ready, 2 * (B - 1))
                transpose_x1(B - 1, (B - 1) % 2)
                pe.wait_ge(relu_ready, B - 1)
                pe.wait_ge(th_ready, B - 1)
                mix_product_k(B - 1, pK_last)
                mix_product_r(B - 1, pR_last)
                pe.wait_ge(rk_ready, B - 1)
                channel_mix_output(B - 1)

            all_steps(pe, step, last_steps)


_INS = ["L0_attn_x", "L0_attn_Wq", "L0_attn_Wk", "L0_attn_Wv", "L0_attn_Wp", "L0_attn_bp",
        "L0_ffn_W_r", "L0_ffn_W_k", "L0_ffn_W_v", "L0_ffn_mu_r", "L0_ffn_mu_k"]


def kernel(**inputs):
    import numpy as _np
    import concourse.bacc as _bacc
    from concourse import mybir as _mybir
    from concourse.bass_utils import run_bass_kernel_spmd as _run

    nc = _bacc.Bacc("TRN2", target_bir_lowering=False, num_devices=1)
    arrays, args = {}, []
    for name in _INS:
        a = _np.ascontiguousarray(inputs[name])
        arrays[f"in_{name}"] = a
        args.append(nc.dram_tensor(f"in_{name}", a.shape, _mybir.dt.from_np(a.dtype), kind="ExternalInput").ap())
    shape = arrays["in_L0_attn_x"].shape
    args.append(nc.dram_tensor("out_0", shape, _mybir.dt.float32, kind="ExternalOutput").ap())
    postln_block_kernel(nc, *args)
    r = _run(nc, [arrays], core_ids=[0])
    return r.results[0]["out_0"]
```
